# Optimizing a Trainium2 kernel written in Bass

```python
import numpy as np
import jax
import jax.numpy as jnp

def _softmax(x, axis=-1):
    return jax.nn.softmax(x, axis=axis)

def _gelu(x):
    return jax.nn.gelu(x, approximate=True)

def _silu(x):
    return jax.nn.silu(x)

def _sigmoid(x):
    return jax.nn.sigmoid(x)

def _layernorm(x, axis=-1, eps=1e-05):
    m = jnp.mean(x, axis=axis, keepdims=True)
    v = jnp.var(x, axis=axis, keepdims=True)
    return (x - m) / jnp.sqrt(v + eps)

def _scatter_add(tgt, idx, src, axis=0):
    return tgt.at[idx].add(src)

def _segment_sum(src, seg, n):
    return jax.ops.segment_sum(src, seg, n)
kernel_name = 'mk_macaron_d1_jaxref_r8_33ad34'

def setup_inputs(seed: int=0):
    np.random.seed(seed)
    _w = jnp.asarray

    def _L0_attn_setup():
        import jax, jax.numpy as jnp
        import numpy as np
        D_MODEL = 256
        NUM_HEADS = 16
        HEAD_DIM = D_MODEL // NUM_HEADS
        SCALE = HEAD_DIM ** (-0.5)
        ALPHA = 1.0
        key = jax.random.key(seed)
        ks = jax.random.split(key, 9)
        B, T = (2, 256)
        s = 0.02
        w = lambda k: jax.random.normal(k, (D_MODEL, D_MODEL), jnp.float32) * s
        b = lambda k: jax.random.normal(k, (D_MODEL,), jnp.float32) * s
        return {'x': jax.random.normal(ks[0], (B, T, D_MODEL), jnp.float32), 'q_w': w(ks[1]), 'q_b': b(ks[2]), 'k_w': w(ks[3]), 'k_b': b(ks[4]), 'v_w': w(ks[5]), 'v_b': b(ks[6]), 'o_w': w(ks[7]), 'o_b': b(ks[8])}
    _L0_attn_in = _L0_attn_setup()

    def _L0_ffn_setup():
        import jax, jax.numpy as jnp
        import numpy as np
        TOPK = 2
        NORM_TOPK = True
        SCALE = 1.0
        EPS = 1e-09
        key = jax.random.key(seed)
        ks = jax.random.split(key, 9)
        h, i, E = (256, 128, 16)
        std = 0.02
        return {'x': jax.random.normal(ks[0], (1, 256, h), jnp.float32), 'Wr': jax.random.normal(ks[1], (E, h), jnp.float32) * std, 'bias': jnp.zeros((E,), jnp.float32), 'Wg': jax.random.normal(ks[2], (E, h, i), jnp.float32) * std, 'Wu': jax.random.normal(ks[3], (E, h, i), jnp.float32) * std, 'Wd': jax.random.normal(ks[4], (E, i, h), jnp.float32) * std, 'sWg': jax.random.normal(ks[5], (h, i), jnp.float32) * std, 'sWu': jax.random.normal(ks[6], (h, i), jnp.float32) * std, 'sWd': jax.random.normal(ks[7], (i, h), jnp.float32) * std}
    _L0_ffn_in = _L0_ffn_setup()
    _d = {'L0_attn_x': _L0_attn_in['x'], 'L0_attn_q_w': _L0_attn_in['q_w'], 'L0_attn_q_b': _L0_attn_in['q_b'], 'L0_attn_k_w': _L0_attn_in['k_w'], 'L0_attn_k_b': _L0_attn_in['k_b'], 'L0_attn_v_w': _L0_attn_in['v_w'], 'L0_attn_v_b': _L0_attn_in['v_b'], 'L0_attn_o_w': _L0_attn_in['o_w'], 'L0_attn_o_b': _L0_attn_in['o_b'], 'L0_ffn_Wr': _L0_ffn_in['Wr'], 'L0_ffn_bias': _L0_ffn_in['bias'], 'L0_ffn_Wg': _L0_ffn_in['Wg'], 'L0_ffn_Wu': _L0_ffn_in['Wu'], 'L0_ffn_Wd': _L0_ffn_in['Wd'], 'L0_ffn_sWg': _L0_ffn_in['sWg'], 'L0_ffn_sWu': _L0_ffn_in['sWu'], 'L0_ffn_sWd': _L0_ffn_in['sWd']}
    _x0 = _d['L0_attn_x']
    _d['L0_attn_x'] = jax.random.normal(jax.random.fold_in(jax.random.key(seed), 1), (2, 512, 256), dtype=_x0.dtype)
    del _x0
    return _d

def reference(L0_attn_x, L0_attn_q_w, L0_attn_q_b, L0_attn_k_w, L0_attn_k_b, L0_attn_v_w, L0_attn_v_b, L0_attn_o_w, L0_attn_o_b, L0_ffn_Wr, L0_ffn_bias, L0_ffn_Wg, L0_ffn_Wu, L0_ffn_Wd, L0_ffn_sWg, L0_ffn_sWu, L0_ffn_sWd):

    def _L0_attn_ref(x, q_w, q_b, k_w, k_b, v_w, v_b, o_w, o_b):
        import jax, jax.numpy as jnp
        import numpy as np
        D_MODEL = 256
        NUM_HEADS = 16
        HEAD_DIM = D_MODEL // NUM_HEADS
        SCALE = HEAD_DIM ** (-0.5)
        ALPHA = 1.0
        B, T, D = x.shape
        H, HD = (NUM_HEADS, HEAD_DIM)

        def proj_split(w, bias):
            y = x @ w.T + bias
            return y.reshape(B, T, H, HD).transpose(0, 2, 1, 3).reshape(B * H, T, HD)
        Q = proj_split(q_w, q_b)
        K = proj_split(k_w, k_b)
        V = proj_split(v_w, v_b)
        S = jnp.einsum('hid,hjd->hij', K, Q) * SCALE
        idx = jnp.arange(T)
        delta = idx[:, None] - idx[None, :]
        decay = jnp.where(delta < 0, 0.0, -delta.astype(jnp.float32) ** ALPHA)
        S = jnp.where(delta < 0, -jnp.inf, S) + decay
        C = jax.nn.softmax(S, axis=-1)
        attn = jnp.einsum('hij,hjd->hid', C, V)
        attn = attn.reshape(B, H, T, HD).transpose(0, 2, 1, 3).reshape(B, T, D)
        return attn @ o_w.T + o_b

    def _L0_ffn_ref(x, Wr, bias, Wg, Wu, Wd, sWg, sWu, sWd):
        import jax, jax.numpy as jnp
        import numpy as np
        TOPK = 2
        NORM_TOPK = True
        SCALE = 1.0
        EPS = 1e-09
        b, s, h = x.shape
        E = Wr.shape[0]
        xt = x.reshape(b * s, h)
        logits = xt @ Wr.T + bias
        probs = jax.nn.softmax(logits, axis=-1)
        topk_val, topk_idx = jax.lax.top_k(probs, TOPK)
        if NORM_TOPK:
            w = topk_val / (jnp.sum(topk_val, axis=-1, keepdims=True) + EPS)
        else:
            w = topk_val
        w = w * SCALE
        g = jnp.einsum('th,ehi->tei', xt, Wg)
        u = jnp.einsum('th,ehi->tei', xt, Wu)
        y = jnp.einsum('tei,eih->teh', jax.nn.silu(g) * u, Wd)
        oh = jax.nn.one_hot(topk_idx, E, dtype=x.dtype)
        routed = jnp.einsum('tke,tk,teh->th', oh, w, y)
        shared = jax.nn.silu(xt @ sWg) * (xt @ sWu) @ sWd
        return (routed + shared).reshape(b, s, h)
    x = L0_attn_x
    x = x + 0.5 * _L0_ffn_ref(_layernorm(x, axis=-1), L0_ffn_Wr, L0_ffn_bias, L0_ffn_Wg, L0_ffn_Wu, L0_ffn_Wd, L0_ffn_sWg, L0_ffn_sWu, L0_ffn_sWd)
    x = x + _L0_attn_ref(_layernorm(x, axis=-1), L0_attn_q_w, L0_attn_q_b, L0_attn_k_w, L0_attn_k_b, L0_attn_v_w, L0_attn_v_b, L0_attn_o_w, L0_attn_o_b)
    x = x + 0.5 * _L0_ffn_ref(_layernorm(x, axis=-1), L0_ffn_Wr, L0_ffn_bias, L0_ffn_Wg, L0_ffn_Wu, L0_ffn_Wd, L0_ffn_sWg, L0_ffn_sWu, L0_ffn_sWd)
    return x

_drawn_inputs = setup_inputs


def setup_inputs(seed=0):
    import zlib

    import numpy as np

    out = dict(_drawn_inputs(seed))
    spreads = {'L0_ffn_bias': (0.0, 0.8)}
    factors = {'L0_attn_q_w': 8.0,
     'L0_attn_q_b': 64.0,
     'L0_attn_k_w': 8.0,
     'L0_attn_k_b': 22.548,
     'L0_attn_v_b': 8.0,
     'L0_attn_o_b': 2.954,
     'L0_ffn_Wr': 7.39,
     'L0_ffn_Wg': 6.784,
     'L0_ffn_Wu': 6.694,
     'L0_ffn_Wd': 6.69,
     'L0_ffn_sWg': 4.845,
     'L0_ffn_sWu': 4.753,
     'L0_ffn_sWd': 4.769}
    for name, (base, spread) in spreads.items():
        noise = np.random.default_rng([zlib.crc32(name.encode()), seed]).standard_normal(out[name].shape)
        drawn = base * np.exp(spread * noise) if base else spread * noise
        out[name] = jnp.asarray(drawn.astype(out[name].dtype))
    for name, factor in factors.items():
        out[name] = (out[name] * factor).astype(out[name].dtype)
    return out
```

```python
from contextlib import ExitStack

import concourse.bass as bass
from concourse import mybir

ALU = mybir.AluOpType
ACT = mybir.ActivationFunctionType
AX = mybir.AxisListType
F32 = mybir.dt.float32
F32R = mybir.dt.float32r
BF16 = mybir.dt.bfloat16
F16 = mybir.dt.float16
I32 = mybir.dt.int32
U32 = mybir.dt.uint32

P = 128
NEG = -3.0e38


def macaron_kernel(nc, x, q_w, k_w, v_w, o_w, qk_b, v_b, o_b, r_w, r_b, experts, out):
    B, SEQ, D = x.shape
    E = experts.shape[0] - 1
    F = experts.shape[2] // 6
    N = B * SEQ
    NT = N // P
    KT = D // P
    NP_ = NT // 2
    H, HD = 16, 16
    QT = SEQ // P
    NB = (2 * N + E * (P - 1)) // P
    G = 4
    NG = B * H // G
    RING = 4
    PEEL = 5
    EPS_LN, EPS_TOP = 1e-5, 1e-9
    WE = KT * 2 * F + D
    GU = 2 * F
    STK = 6 * HD
    VW = HD + 1
    assert (P, KT, F, NB, QT) == (128, 2, 128, 31, 4)

    x_v = x.rearrange("b (t p) d -> p (b t) d", p=P)
    out_v = out.rearrange("b (t p) d -> p (b t) d", p=P)
    slots_x = nc.dram_tensor("slots_x", (NB * P, D), F32, kind="Internal").ap()
    slots_y = nc.dram_tensor("slots_y", (NB * P, D), F32, kind="Internal").ap()
    parts_d = nc.dram_tensor("parts_d", (2, 3, D, N), BF16, kind="Internal").ap()

    with ExitStack() as ctx:
        def sb(name, shape, dt=F32, to=ctx):
            return to.enter_context(nc.sbuf_tensor(name, shape, dt))

        def sem(name):
            return ctx.enter_context(nc.semaphore(name))

        bank = [ctx.enter_context(nc.psum_tensor(f"bank{i}", [P, 512], F32)) for i in range(8)]

        wh = sb("wh", [P, E + 1, WE], F32R)
        wl = sb("wl", [P, E + 1, WE], F32R)
        rw = [sb(f"rw_{i}", [P, KT, E], F32R) for i in "hl"]
        rw_s = sb("rw_s", [P, KT, E])
        res = sb("res", [P, NT, D])
        xn = sb("xn", [P, NT, D])
        att = xn
        ident = sb("ident", [P, P])
        ident_b = sb("ident_b", [P, P], BF16)
        ones_b = sb("ones_b", [P, P], BF16)
        below_b = sb("below_b", [P, P], BF16)
        stats = sb("stats", [P, NT, 6])
        mv = sb("mv", [P, NT, 2])
        rstd = sb("rstd", [P, NT])
        dev = sb("dev", [P, NT])
        eps = sb("eps", [P, 1])
        dec = sb("dec", [P, 512])
        dec_d = sb("dec_d", [P, P], BF16)
        dec_o = sb("dec_o", [P, 3 * P], F16)
        qkb = sb("qkb", [P, 2, KT])
        vb = sb("vb", [P, D])
        ob = sb("ob", [P, D])
        rb = sb("rb", [P, E])
        dn = sb("dn", [P, E])
        kk = sb("kk", [P, NT])
        lt = sb("lt", [P, E, E], BF16)
        bno = sb("bno", [1, NB])
        mx = sb("mx", [P, NT])
        rsum = sb("rsum", [P, NT])
        top = sb("top", [P, 2, NT])
        fst = sb("fst", [P, NT])
        gate = sb("gate", [P, 2, NT])
        nblk = sb("nblk", [P, E])
        base = sb("base", [P, E])
        incl = sb("incl", [1, E])
        bex = sb("bex", [1, NB])
        bexi = sb("bexi", [1, NB + 1], I32)
        slot = sb("slot", [P, 2, NT], U32)

        r1 = ExitStack()
        xnT = [sb(f"xnT_{i}", [P, KT, N], F32R, r1) for i in "hl"]
        stg = [sb(f"stg{i}", [P, WE], F32, r1) for i in range(4)]
        zeros = sb("zeros", [P, D], F32, r1)
        r1.close()
        r1 = ExitStack()
        sb("below_wa", [P, 2 * KT * N], F32, r1)
        wa_s = sb("wa_s", [P, KT, D], F32, r1)
        wa = [[sb(f"wa{j}_{i}", [P, KT, D], F32R, r1) for i in "hl"] for j in "qkv"]
        r1.close()
        ct = [sb(f"ct{i}", [P, 1280]) for i in range(6)]
        r2 = ExitStack()
        yg = [sb(f"yg{i}", [P, 2, D], F32, r2) for i in range(4)]
        xb = [sb(f"xb{i}", [P, D], F32, r2) for i in range(RING)]
        xT = [[sb(f"xT{j}_{i}", [P, KT, P], F32R, r2) for i in "hl"] for j in range(2)]
        sg = [sb(f"sg{i}", [P, F], F32, r2) for i in range(2)]
        hm = [sb(f"hm{i}", [P, F], F32, r2) for i in range(2)]
        hT = [[sb(f"hT{j}_{i}", [P, P], F32R, r2) for i in "hl"] for j in range(2)]
        ysb = [sb(f"ysb{i}", [P, D], F32, r2) for i in range(RING)]
        lg = sb("lg", [P, NT, E], F32, r2)
        pr = sb("pr", [P, NT, E], F32, r2)
        tmp = sb("tmp", [P, NT, E], F32, r2)
        oh = sb("oh", [P, 2, NT, E], F32, r2)
        ohs = sb("ohs", [P, NT, E], BF16, r2)
        big = sb("big", [P, NB * E], F32, r2)
        iota_i = sb("iota_i", [P, 512], I32, r2)
        r2.close()
        stk_k = [sb(f"stk_k{i}", [STK + 2, G, SEQ], BF16) for i in range(3)]
        stk_q = [sb(f"stk_q{i}", [STK + 2, G, SEQ], BF16) for i in range(3)]
        r3 = ExitStack()
        pf = [sb(f"pf{i}", [P, 512], F32, r3) for i in range(2)]
        pq = [sb(f"pq{i}", [P, 512], F32, r3) for i in range(2)]
        part = [[sb(f"part{j}_{i}", [P, 512], BF16, r3) for i in "hml"] for j in range(2)]
        r3.close()
        r3 = ExitStack()
        osb = [sb(f"osb{i}", [P, 512], F32, r3) for i in range(2)]
        wo = [sb(f"wo_{i}", [P, KT, D], F32R, r3) for i in "hl"]
        wo_s = sb("wo_s", [P, KT, D], F32, r3)
        junk = [sb(f"junk{i}", [P, 512], BF16, r3) for i in range(2)]
        negm = [sb(f"negm{i}", [P, 2, G * QT], BF16, r3) for i in range(2)]
        mmax = [sb(f"mmax{i}", [P, G * QT], F32, r3) for i in range(2)]
        mT = [sb(f"mT{i}", [2 * G * QT, P], BF16, r3) for i in range(2)]
        rc = sb("rc", [P, QT, G], F32, r3)
        r3.close()
        sb("below_v", [P, 3584], F32)
        V = sb("V", [P, NT, H * VW + 16])

        s_x = [sem(f"s_x{r}") for r in range(NP_)]
        s_small = sem("s_small")
        s_const = sem("s_const")
        s_stg = [sem(f"s_stg{i}") for i in range(4)]
        s_whi = sem("s_whi")
        s_wlo_p = sem("s_wlo_p")
        s_wlo_v = sem("s_wlo_v")
        s_rw = sem("s_rw")
        s_zero = sem("s_zero")
        s_fill = sem("s_fill")
        s_dv = sem("s_dv")
        s_pool = sem("s_pool")
        s_mv = sem("s_mv")
        s_dev = sem("s_dev")
        s_xn = sem("s_xn")
        s_tr = sem("s_tr")
        s_thi = sem("s_thi")
        s_tlo = sem("s_tlo")
        s_rt = sem("s_rt")
        s_lg = sem("s_lg")
        s_ex = sem("s_ex")
        s_oh = sem("s_oh")
        s_rk = sem("s_rk")
        s_slot = sem("s_slot")
        s_sc = sem("s_sc")
        s_xb = [sem(f"s_xb{i}") for i in range(RING)]
        s_xt = sem("s_xt")
        s_xth = sem("s_xth")
        s_xtl = sem("s_xtl")
        s_gu = sem("s_gu")
        s_sg = sem("s_sg")
        s_hm = sem("s_hm")
        s_ht = sem("s_ht")
        s_hth = sem("s_hth")
        s_htl = sem("s_htl")
        s_y = sem("s_y")
        s_ysh = sem("s_ysh")
        s_ye = sem("s_ye")
        s_ys = [sem(f"s_ys{i}") for i in range(RING)]
        s_yg = [sem(f"s_yg{i}") for i in range(4)]
        s_cmb = sem("s_cmb")
        s_was = sem("s_was")
        s_wap = sem("s_wap")
        s_qkb = sem("s_qkb")
        s_vone = sem("s_vone")
        s_ones = sem("s_ones")
        s_resb = sem("s_resb")
        s_qk = sem("s_qk")
        s_pf = sem("s_pf")
        s_ph = sem("s_ph")
        s_pm = sem("s_pm")
        s_pl = sem("s_pl")
        s_pd = [sem(f"s_pd{i}") for i in range(8)]
        s_vp = sem("s_vp")
        s_v = sem("s_v")
        s_stk = [sem(f"s_stk{i}") for i in range(3)]
        s_s = sem("s_s")
        s_max = sem("s_max")
        s_nm = sem("s_nm")
        s_mt = sem("s_mt")
        s_mts = sem("s_mts")
        s_mr = [sem(f"s_mr{i}") for i in range(2)]
        s_st = sem("s_st")
        s_exp = sem("s_exp")
        s_pv = sem("s_pv")
        s_ot = sem("s_ot")
        s_otr = sem("s_otr")
        s_att = sem("s_att")
        s_wos = sem("s_wos")
        s_wo = sem("s_wo")
        s_o = sem("s_o")
        s_res2 = sem("s_res2")
        s_out = sem("s_out")

        order = [E] + list(range(E))
        POOL_PREPS = 8
        NJ = NT + NB
        off = [0, 512, 1024, 896]
        LEAD = 6
        NH = B * H
        NS_CONST = 19

        def three(eng, to, xs, ws, ins):
            terms = [(k, a, b) for k in range(KT) for a, b in ((0, 0), (0, 1), (1, 0))] if ins is None else ins
            for i, (k, a, b) in enumerate(terms):
                mm = eng.matmul(to, xs(k, a), ws(k, b), start=i == 0, stop=i == len(terms) - 1)
            return mm

        def back(q, r, k):
            return q + (r - k) // RING, (r - k) % RING

        def over_blocks(step):
            for b in range(NB + 3):
                step(b, [0 <= b - k < NB for k in range(4)])

        block = ctx.enter_context(nc.Block())

        @block.sync
        def _(sp):
            def load_x(r):
                sp.dma_start(res[:, 2 * r:2 * r + 2, :], x_v[:, 2 * r:2 * r + 2, :]).then_inc(s_x[r], 16)

            def load_expert(q):
                if q >= 4:
                    sp.wait_ge(s_whi, q - 3)
                    if q - 4 < POOL_PREPS:
                        sp.wait_ge(s_wlo_p, q - 3)
                    else:
                        sp.wait_ge(s_wlo_v, q - 3 - POOL_PREPS)
                sp.dma_start(stg[q % 4][:], experts[order[q]]).then_inc(s_stg[q % 4], 16)

            for r in range(NP_):
                load_x(r)
            sp.dma_start(rw_s[:], r_w).then_inc(s_small, 16)
            sp.dma_start(rb[:], r_b.partition_broadcast(P)).then_inc(s_small, 16)
            sp.dma_start(qkb[:], qk_b).then_inc(s_small, 16)
            sp.dma_start(vb[:], v_b.partition_broadcast(P)).then_inc(s_small, 16)
            sp.dma_start(ob[:], o_b.partition_broadcast(P)).then_inc(s_small, 16)
            for q in range(3):
                load_expert(q)
            sp.wait_ge(s_zero, 2)
            sp.dma_start(slots_x.rearrange("(p a) d -> p a d", p=P),
                         zeros[:, None, :].to_broadcast([P, NB, D])).then_inc(s_fill, 16)
            for q in range(3, E + 1):
                load_expert(q)

            def blocks(f):
                def load(q, r):
                    sp.dma_start(xb[r][:], slots_x[bass.ds((q * RING + r) * P, P), :]).then_inc(s_xb[r], 16)

                def step(q, r, live):
                    if live[0]:
                        sp.wait_ge(s_xt, q * RING + (r + f * NB + 1))
                        if not isinstance(q, int) or q * RING + r + RING < NB:
                            load(q + 1, r)
                    if live[3]:
                        q3, r3 = back(q, r, 3)
                        sp.wait_ge(s_ye, q3 * RING + (r3 + f * NB + 1))
                        sp.dma_start(slots_y[bass.ds((q3 * RING + r3) * P, P), :], ysb[r3][:]).then_inc(s_ys[r3], 16)

                sp.wait_ge(s_sc, 16 * 2 * NT * (f + 1))
                for b in range(RING):
                    load(0, b)
                turns_ = (NB - PEEL - RING) // RING
                for i in range(PEEL):
                    step(0 + i // RING, i % RING, [0 <= i - k for k in range(4)])
                with sp.Fori(0, turns_) as n:
                    for i in range(PEEL, PEEL + RING):
                        step(n + i // RING, i % RING, [True] * 4)
                for i in range(PEEL + turns_ * RING, NB + 3):
                    step(i // RING, i % RING, [0 <= i - k < NB for k in range(4)])

            def attention():
                def store_parts(it):
                    sp.wait_ge(s_ph, it + 1)
                    sp.wait_ge(s_pm, it + 1)
                    sp.wait_ge(s_pl, it + 1)
                    c, m, op = it // 4, it // 2 % 2, it % 2
                    for i in range(3):
                        sp.dma_start(parts_d[op, i, m * P:(m + 1) * P, c * SEQ:(c + 1) * SEQ],
                                     part[it % 2][i][:]).then_inc(s_pd[it], 16)

                def load_stacks(g):
                    c, hg = g // 4, g % 4
                    for it in (4 * c + hg // 2 * 2, 4 * c + hg // 2 * 2 + 1):
                        sp.wait_ge(s_pd[it], 48)
                    if g >= 3:
                        sp.wait_ge(s_st, 3 * G * (g - 2))
                    for op, stk, parts in ((1, stk_k, (0, 0, 0, 1, 1, 2)), (0, stk_q, (0, 1, 2, 0, 1, 0))):
                        for i, a in enumerate(parts):
                            src = parts_d[op, a, hg * G * HD:(hg + 1) * G * HD, c * SEQ:(c + 1) * SEQ]
                            sp.dma_start(stk[g % 3][i * HD:(i + 1) * HD, :, :],
                                         src.rearrange("(h d) t -> d h t", d=HD)).then_inc(s_stk[g % 3], 16)

                def store_maxima(g):
                    sp.wait_ge(s_mts, g + 1)
                    for a in range(2):
                        dst = stk_k[g % 3][STK + a:STK + a + 1, :, :].rearrange("o u (i t) -> o (u i) t", t=P)
                        sp.dma_start(dst, mT[g % 2][a * G * QT:(a + 1) * G * QT, :]).then_inc(s_mr[g % 2], 16)

                for it in range(4):
                    store_parts(it)
                load_stacks(0)
                load_stacks(1)
                for it in range(4, 8):
                    store_parts(it)
                load_stacks(2)
                store_maxima(0)
                store_maxima(1)
                for g in range(3, NG):
                    load_stacks(g)
                    store_maxima(g - 1)
                store_maxima(NG - 1)

            blocks(0)
            attention()
            blocks(1)
            for t in range(NT):
                sp.wait_ge(s_cmb, NT + t + 1)
                sp.dma_start(out_v[:, t, :], res[:, t, :]).then_inc(s_out, 16)
            sp.wait_ge(s_out, 16 * NT)

        @block.gpsimd
        def _(pool):
            steps = [0]

            def link(ins):
                steps[0] += 1
                ins.then_inc(s_pool, 1)
                pool.wait_ge(s_pool, steps[0])

            pool.memset(eps[:], EPS_LN).then_inc(s_zero, 1)
            pool.memset(zeros[:], 0.0).then_inc(s_zero, 1)
            link(pool.memset(ident[:], 0.0))
            pool.affine_select(out=ident[:], in_=ident[:], compare_op=ALU.not_equal, fill=1.0, base=0,
                               pattern=[[-1, P]], channel_multiplier=1).then_inc(s_const, 1)

            link(pool.iota(iota_i[:, 0:E], pattern=[[-1, E]], base=E, channel_multiplier=0))
            link(pool.tensor_copy(dn[:], iota_i[:, 0:E]))
            link(pool.iota(iota_i[:, 0:NT], pattern=[[P, NT]], base=0, channel_multiplier=0))
            link(pool.tensor_copy(kk[:], iota_i[:, 0:NT]))
            link(pool.iota(iota_i[0:1, 0:NB], pattern=[[1, NB]], base=0, channel_multiplier=0))
            link(pool.tensor_copy(bno[:], iota_i[0:1, 0:NB]))
            link(pool.memset(lt[:], 1.0))
            link(pool.affine_select(out=lt[:], in_=lt[:], compare_op=ALU.is_gt, fill=0.0, base=0,
                                    pattern=[[1, E], [-1, E]], channel_multiplier=0))
            link(pool.memset(ones_b[:], 1.0))
            link(pool.affine_select(out=below_b[:], in_=ones_b[:], compare_op=ALU.is_gt, fill=0.0, base=0,
                                    pattern=[[1, P]], channel_multiplier=-1))
            pool.tensor_copy(ident_b[:], ident[:]).then_inc(s_const, 1)

            def split_low(q):
                e = order[q]
                pool.wait_ge(s_whi, q + 1)
                pool.tensor_tensor(wl[:, e, :], stg[q % 4][:], wh[:, e, :].bitcast(F32), ALU.subtract)\
                    .then_inc(s_wlo_p, 1)

            for q in range(POOL_PREPS):
                split_low(q)

            def scatter(f):
                pool.wait_ge(s_slot, f + 1)
                if f == 0:
                    pool.wait_ge(s_fill, 16)
                for t in range(NT):
                    for k in range(2):
                        pool.indirect_dma_start(slots_x, bass.IndirectOffsetOnAxis(ap=slot[:, k, t:t + 1], axis=0),
                                                xn[:, t, :], None).then_inc(s_sc, 16)

            def gather(f):
                for r in range(RING):
                    uses = (NB - r + RING - 1) // RING
                    pool.wait_ge(s_ys[r], 16 * uses * (f + 1))
                for t in range(NT):
                    if t >= 4:
                        pool.wait_ge(s_cmb, NT * f + t - 3)
                    for k in range(2):
                        pool.indirect_dma_start(yg[t % 4][:, k, :], None, slots_y,
                                                bass.IndirectOffsetOnAxis(ap=slot[:, k, t:t + 1], axis=0))\
                            .then_inc(s_yg[t % 4], 16)

            scatter(0)
            pool.wait_ge(s_small, 80)
            pool.tensor_scalar(qkb[:, 0, :], qkb[:, 0, :], HD ** -0.5, None, ALU.mult).then_inc(s_qkb, 1)
            pool.memset(V[:], 1.0).then_inc(s_vone, 1)
            pool.wait_ge(s_slot, 1)
            link(pool.iota(iota_i[:], pattern=[[1, 512]], base=-384, channel_multiplier=-1))
            link(pool.tensor_copy(dec[:], iota_i[:]))
            link(pool.affine_select(out=dec[:], in_=dec[:], compare_op=ALU.is_ge, fill=NEG, base=384,
                                    pattern=[[-1, 512]], channel_multiplier=1))
            link(pool.iota(iota_i[:, 0:P], pattern=[[-1, P]], base=0, channel_multiplier=1))
            link(pool.tensor_copy(dec_d[:], iota_i[:, 0:P]))
            link(pool.affine_select(out=dec_d[:], in_=dec_d[:], compare_op=ALU.is_ge, fill=NEG, base=0,
                                    pattern=[[1, P]], channel_multiplier=-1))
            link(pool.iota(iota_i[:, 0:3 * P], pattern=[[-1, 3 * P]], base=-P, channel_multiplier=1))
            pool.tensor_copy(dec_o[:], iota_i[:, 0:3 * P]).then_inc(s_const, 1)
            pool.wait_ge(s_wlo_v, E + 1 - POOL_PREPS)
            for j, w in enumerate((q_w, k_w, v_w)):
                pool.dma_start(wa_s[:], w).then_inc(s_was, 16)
                pool.wait_ge(s_was, 16 * (j + 1))
                link(pool.tensor_copy(wa[j][0][:], wa_s[:]))
                link(pool.tensor_tensor(wa[j][1][:], wa_s[:], wa[j][0][:].bitcast(F32), ALU.subtract))
            pool.nop().then_inc(s_wap, 1)
            gather(0)

            pool.wait_ge(s_xn, 2 * NP_)
            for i in range(3):
                pool.memset(stk_q[i][STK:STK + 2, :, :], 1.0).then_inc(s_ones, 1)
            pool.wait_ge(s_ones, 3)
            for it in range(8):
                pool.wait_ge(s_pm, it + 1)
                if it >= 2:
                    pool.wait_ge(s_pd[it - 2], 48)
                pool.tensor_tensor(part[it % 2][2][:], pq[it % 2][:], part[it % 2][1][:], ALU.subtract)\
                    .then_inc(s_pl, 1)
            for t in range(NT):
                pool.tensor_tensor(res[:, t, :], res[:, t, :], ob[:], ALU.add).then_inc(s_resb, 1)
            for it in (6, 7):
                pool.wait_ge(s_pd[it], 48)
            pool.dma_start(wo_s[:], o_w).then_inc(s_wos, 16)
            pool.wait_ge(s_wos, 16)
            link(pool.tensor_copy(wo[0][:], wo_s[:]))
            pool.tensor_tensor(wo[1][:], wo_s[:], wo[0][:].bitcast(F32), ALU.subtract).then_inc(s_wo, 1)

            scatter(1)
            gather(1)

        @block.scalar
        def _(act):
            def split_high(q):
                e = order[q]
                act.wait_ge(s_stg[q % 4], 16 * (q // 4 + 1))
                act.activation(wh[:, e, :], stg[q % 4][:], ACT.Copy).then_inc(s_whi, 1)

            def turns(n):
                for r in range(-2, NP_):
                    if n != 2 and r + 2 < NP_:
                        act.wait_ge(s_mv, NP_ * (n - n // 2) + r + 3)
                        act.activation(dev[:, 2 * r + 4:2 * r + 6], mv[:, 2 * r + 4:2 * r + 6, 1], ACT.Sqrt,
                                       bias=eps[:]).then_inc(s_dev, 1)
                    if r < 0:
                        continue
                    act.wait_ge(s_tr, NP_ * n + r + 1)
                    src = bank[r % 2][:].rearrange("p (k t) -> p k t", k=KT)
                    act.activation(xnT[0][:, :, 2 * P * r:2 * P * (r + 1)], src, ACT.Copy).then_inc(s_thi, 1)

            def hidden(j, par, first):
                act.wait_ge(s_gu, j + 1)
                if not first:
                    act.wait_ge(s_hm, j - 1)
                act.activation(sg[par][:], bank[2 + par][:, 0:F], ACT.Silu).then_inc(s_sg, 1)

            def hidden_high(j, par, first):
                act.wait_ge(s_ht, j + 1)
                if not first:
                    act.wait_ge(s_y, j - 1)
                act.activation(hT[par][0][:], bank[4 + par][:, 0:P], ACT.Copy).then_inc(s_hth, 1)

            def ffn(f):
                act.wait_ge(s_lg, f + 1)
                act.activation(pr[:], lg[:], ACT.Exp).then_inc(s_ex, 1)
                for i in range(NT + 2):
                    if i < NT:
                        hidden(f * NJ + i, (f * NJ + i) % 2, i < 2 and not f)
                    if 0 <= i - 1 < NT:
                        hidden_high(f * NJ + i - 1, (f * NJ + i - 1) % 2, i - 1 < 2 and not f)
                if f == 0:
                    for q in range(POOL_PREPS, E + 1):
                        split_high(q)

                def step(b, live):
                    j = f * NJ + NT + b
                    if live[0]:
                        act.wait_ge(s_xt, f * NB + b + 1)
                        if b < 2:
                            act.wait_ge(s_gu, j - 1)
                        act.activation(xT[b % 2][0][:], bank[b % 2][:, 0:D].rearrange("p (k t) -> p k t", k=KT),
                                       ACT.Copy).then_inc(s_xth, 1)
                    if live[1]:
                        hidden(j - 1, (j - 1) % 2, False)
                    if live[2]:
                        hidden_high(j - 2, j % 2, False)

                over_blocks(step)

            act.wait_ge(s_small, 80)
            act.wait_ge(s_zero, 2)
            act.activation(rw[0][:], rw_s[:], ACT.Copy).then_inc(s_rw, 1)
            turns(0)
            for q in range(POOL_PREPS):
                split_high(q)
            ffn(0)

            turns(1)
            act.wait_ge(s_qkb, 1)
            for it in range(8):
                m, op = it // 2 % 2, it % 2
                act.wait_ge(s_qk, it + 1)
                if it >= 2:
                    act.wait_ge(s_pm, it - 1)
                act.activation(pf[it % 2][:], bank[2 + it % 2][:], ACT.Identity, bias=qkb[:, op, m:m + 1],
                               scale=1.0 if op else HD ** -0.5).then_inc(s_pf, 1)
                act.wait_ge(s_pf, it + 1)
                if it >= 2:
                    act.wait_ge(s_pd[it - 2], 48)
                act.activation(part[it % 2][0][:], pf[it % 2][:], ACT.Copy).then_inc(s_ph, 1)

            def out_of_v(g):
                act.wait_ge(s_pv, g + 1)
                if g >= 2:
                    act.wait_ge(s_otr, g - 1)
                if g == 0:
                    act.wait_ge(s_pd[7], 48)
                    act.wait_ge(s_pl, 8)
                act.activation(osb[g % 2][:], bank[6][:], ACT.Copy).then_inc(s_ot, 1)

            for n in range(NH):
                for i, (a, b) in enumerate(((0, 512), (512, 1024), (1024, 1280))):
                    act.wait_ge(s_st, 3 * n + i + 1)
                    if n >= 6 and i == 0:
                        act.wait_ge(s_pv, (n - 6) // G + 1)
                    act.activation(ct[n % 6][:, a:b], bank[2 + i][:, 0:b - a], ACT.Exp).then_inc(s_exp, 1)
                if n % G == 1 and n > G:
                    out_of_v(n // G - 1)
            out_of_v(NG - 1)
            turns(2)
            turns(3)
            ffn(1)

        @block.tensor
        def _(pe):
            def turns(n, ready):
                for r in range(NP_):
                    ready(r)
                    if r >= 2:
                        pe.wait_ge(s_tlo, NP_ * n + r - 1)
                    for k in range(KT):
                        for t in range(2):
                            mm = pe.transpose(bank[r % 2][:, (2 * k + t) * P:(2 * k + t + 1) * P],
                                              xn[:, 2 * r + t, k * P:(k + 1) * P], ident[:])
                    mm.then_inc(s_tr, 1)

            def rows(t):
                return lambda k, a: xnT[a][:, k, t * P:(t + 1) * P]

            def gate_up(j, par, first, xs, ws):
                if not first:
                    pe.wait_ge(s_hm, j - 1)
                three(pe, bank[2 + par][:, 0:GU], xs, ws, None).then_inc(s_gu, 1)

            def hidden_turn(j, par, first):
                pe.wait_ge(s_hm, j + 1)
                if not first:
                    pe.wait_ge(s_htl, j - 1)
                pe.transpose(bank[4 + par][:, 0:P], hm[par][:], ident[:]).then_inc(s_ht, 1)

            def down(j, par, wd):
                pe.wait_ge(s_htl, j + 1)
                three(pe, bank[6 + par][:, 0:D], lambda k, a: hT[par][a][:], lambda k, b: wd(b),
                      [(0, 0, 0), (0, 0, 1), (0, 1, 0)]).then_inc(s_y, 1)

            def ffn(f, n):
                for t in range(NT):
                    if t % 2 == 0:
                        pe.wait_ge(s_tlo, NP_ * n + t // 2 + 1)
                    mm = three(pe, bank[2][:, t * E:(t + 1) * E], rows(t), lambda k, b: rw[b][:, k, :], None)
                mm.then_inc(s_rt, 1)
                pe.wait_ge(s_oh, f + 1)
                flat = ohs[:].rearrange("p t e -> p (t e)")
                pe.matmul(bank[3][:, 0:NT * E], below_b[:], flat, start=True, stop=False, skip_group_check=True)
                for s in range(1, NT):
                    pe.matmul(bank[3][:, s * E:NT * E], ones_b[:], flat[:, 0:(NT - s) * E], start=False,
                              stop=s == NT - 1, skip_group_check=True)
                for t in range(NT):
                    mm = pe.matmul(bank[4][:, 0:E], ones_b[:], flat[:, t * E:(t + 1) * E], start=t == 0,
                                   stop=t == NT - 1)
                mm.then_inc(s_rk, 1)
                if f == 0:
                    pe.wait_ge(s_wlo_p, 1)
                pe.wait_ge(s_slot, f + 1)

                def w_s(k, b):
                    return (wh, wl)[b][:, E, k * GU:(k + 1) * GU]

                for i in range(NT + 2):
                    j = f * NJ + i
                    if i < NT:
                        gate_up(j, j % 2, f == 0 and i < 2, rows(i), w_s)
                    if 0 <= i - 1 < NT:
                        hidden_turn(j - 1, (j - 1) % 2, f == 0 and i - 1 < 2)
                    if 0 <= i - 2 < NT:
                        if i - 2 >= 2:
                            pe.wait_ge(s_ysh, f * NT + i - 3)
                        down(j - 2, j % 2, lambda b: (wh, wl)[b][:, E, KT * GU:WE])
                pe.wait_ge(s_ysh, (f + 1) * NT)
                pe.wait_ge(s_wlo_v, E + 1 - POOL_PREPS)
                pe.wait_ge(s_wlo_p, POOL_PREPS)

                whl = [w[:].rearrange("p e n -> p (e n)") for w in (wh, wl)]
                at = {}

                def step(b, live):
                    j, n = f * NJ + NT + b, f * NB + b
                    if b % RING == 0 and b < NB:
                        regs = [pe.alloc_register(f"expert{f}_{i}") for i in range(b, min(b + RING, NB))]
                        pe.load(regs, bexi[0:1, b:b + len(regs)])
                        for i, reg in enumerate(regs):
                            at[b + i] = pe.snap(reg, donate=True, min_val=0, max_val=(E - 1) * WE)
                    if live[0]:
                        pe.wait_ge(s_xb[b % RING], 16 * (f * ((NB - b % RING + RING - 1) // RING) + b // RING + 1))
                        if b < 2 and f:
                            pe.wait_ge(s_xtl, n - 1)
                        for k in range(KT):
                            mm = pe.transpose(bank[b % 2][:, k * P:(k + 1) * P],
                                              xb[b % RING][:, k * P:(k + 1) * P], ident[:])
                        mm.then_inc(s_xt, 1)
                    if live[1]:
                        pe.wait_ge(s_xtl, n)
                        gate_up(j - 1, (j - 1) % 2, b - 1 >= 2, lambda k, a: xT[(b - 1) % 2][a][:, k, :],
                                lambda k, c: whl[c][:, bass.ds(at[b - 1] + k * GU, GU)])
                    if live[2]:
                        hidden_turn(j - 2, j % 2, b - 2 >= 2)
                    if live[3]:
                        if f or b >= 5:
                            pe.wait_ge(s_ye, n - 4)
                        down(j - 3, (j - 3) % 2, lambda c: whl[c][:, bass.ds(at[b - 3] + KT * GU, D)])

                over_blocks(step)

            pe.wait_ge(s_const, 1)
            turns(0, lambda r: pe.wait_ge(s_xn, r + 1))
            pe.wait_ge(s_rw, 2)
            pe.wait_ge(s_const, 2)
            ffn(0, 0)

            turns(1, lambda r: pe.wait_ge(s_xn, NP_ + r + 1))
            pe.wait_ge(s_tlo, 2 * NP_)
            pe.wait_ge(s_wap, 1)
            for it in range(8):
                c, m, op = it // 4, it // 2 % 2, it % 2
                if it >= 2:
                    pe.wait_ge(s_pf, it - 1)
                three(pe, bank[2 + it % 2][:], lambda k, a: wa[op][a][:, k, m * P:(m + 1) * P],
                      lambda k, b: xnT[b][:, k, c * SEQ:(c + 1) * SEQ], None).then_inc(s_qk, 1)
            for t in range(NT):
                if t >= 2:
                    pe.wait_ge(s_v, t - 1)
                three(pe, bank[4 + t % 2][:, 0:D], rows(t), lambda k, b: wa[2][b][:, k, :], None).then_inc(s_vp, 1)

            def score(n, i):
                g, u, num = n // G, n % G, QT * n + QT - 1 - i
                if n % G == 0 and i == QT - 1:
                    pe.wait_ge(s_stk[g % 3], 192 * (g // 3 + 1))
                if num >= 2:
                    pe.wait_ge(s_max, num - 1)
                pe.matmul(bank[num % 2][:, 0:(i + 1) * P], stk_k[g % 3][0:STK, u, i * P:(i + 1) * P],
                          stk_q[g % 3][0:STK, u, 0:(i + 1) * P], start=True, stop=True).then_inc(s_s, 1)

            def scores_t(n, i):
                g, u = n // G, n % G
                if n % G == 0 and i == 0:
                    pe.wait_ge(s_mr[g % 2], 32 * (g // 2 + 1))
                if n >= 1:
                    pe.wait_ge(s_exp, 3 * (n - 1) + i + 1)
                for j, at in (((0, 0),), ((1, 0), (3, 384)), ((2, 0),))[i]:
                    w = SEQ - j * P
                    pe.matmul(bank[2 + i][:, at:at + P], ident_b[:], dec_d[:], start=True, stop=False,
                              skip_group_check=True)
                    if w > P:
                        pe.matmul(bank[2 + i][:, at + P:at + w], ident_b[:], dec_o[:, 0:w - P], start=False,
                                  stop=False, skip_group_check=True)
                    mm = pe.matmul(bank[2 + i][:, at:at + w], stk_q[g % 3][0:STK + 2, u, j * P:(j + 1) * P],
                                   stk_k[g % 3][0:STK + 2, u, j * P:SEQ], start=False, stop=True,
                                   skip_group_check=True)
                mm.then_inc(s_st, 1)

            def maxima_turn(g):
                pe.wait_ge(s_nm, g + 1)
                if g >= 1:
                    pe.wait_ge(s_mts, g)
                pe.transpose(bank[5][:].bitcast(BF16)[0:2 * G * QT, 0:P], negm[g % 2][:].rearrange("p a n -> p (a n)"),
                             ident_b[:]).then_inc(s_mt, 1)

            def times_v(g):
                c, hg = g // 4, g % 4
                pe.wait_ge(s_exp, 3 * G * (g + 1))
                if g >= 1:
                    pe.wait_ge(s_ot, g)
                for j in range(QT):
                    for u in range(G):
                        n, h = G * g + u, G * hg + u
                        mm = pe.matmul(bank[6][32 * u:32 * u + 32, j * P:SEQ],
                                       V[:, c * QT + j, h * VW:h * VW + 32],
                                       ct[n % 6][:, off[j]:off[j] + SEQ - j * P], start=j == 0, stop=j == QT - 1,
                                       skip_group_check=True)
                mm.then_inc(s_pv, 1)

            def out_turn(g):
                pe.wait_ge(s_ot, g + 1)
                if g >= 1:
                    pe.wait_ge(s_att, g)
                for i in range(QT):
                    mm = pe.transpose(bank[7][:, i * P:(i + 1) * P], osb[g % 2][:, i * P:(i + 1) * P], ident[:])
                mm.then_inc(s_otr, 1)

            pe.wait_ge(s_pf, 8)
            pe.wait_ge(s_v, NT)
            pe.wait_ge(s_const, 3)
            for n in range(-LEAD, NH + G):
                ahead = n + LEAD
                if n == 0:
                    pe.wait_ge(s_ones, 3)
                for i in range(QT):
                    if 0 <= ahead < NH:
                        score(ahead, QT - 1 - i)
                    if 0 <= n < NH and i < 3:
                        scores_t(n, i)
                    if i == 1 and ahead % G == 0 and G <= ahead <= NH:
                        maxima_turn(ahead // G - 1)
                if n % G == 0 and G <= n <= NH:
                    times_v(n // G - 1)
                if n % G == 3 and n > G:
                    out_turn(n // G - 1)

            turns(2, lambda r: pe.wait_ge(s_att, 4 * (r // 2 + 1)))
            pe.wait_ge(s_tlo, 3 * NP_)
            pe.wait_ge(s_wo, 1)
            for t in range(NT):
                if t >= 2:
                    pe.wait_ge(s_res2, t - 1)
                three(pe, bank[2 + t % 2][:, 0:D], rows(t), lambda k, b: wo[b][:, k, :], None).then_inc(s_o, 1)
            turns(3, lambda r: pe.wait_ge(s_xn, 2 * NP_ + r + 1))
            ffn(1, 3)

        @block.vector
        def _(dve):
            steps = [0]

            def link(ins):
                steps[0] += 1
                ins.then_inc(s_dv, 1)
                dve.wait_ge(s_dv, steps[0])

            def split_low(q):
                e = order[q]
                dve.wait_ge(s_whi, q + 1)
                dve.tensor_tensor(wl[:, e, :], stg[q % 4][:], wh[:, e, :].bitcast(F32), ALU.subtract)\
                    .then_inc(s_wlo_v, 1)

            def norm(n, ready):
                for r in range(NP_ + 1):
                    if r < NP_:
                        ready(r)
                        for t in (2 * r, 2 * r + 1):
                            ins = dve.bn_stats(stats[:, t, :], res[:, t, :])
                        link(ins)
                        for t in (2 * r, 2 * r + 1):
                            ins = dve.bn_aggr(mv[:, t, :], stats[:, t, :])
                        ins.then_inc(s_mv, 1)
                    if r:
                        dve.wait_ge(s_dev, NP_ * n + r)
                        link(dve.reciprocal(rstd[:, 2 * r - 2:2 * r], dev[:, 2 * r - 2:2 * r]))
                        for t in (2 * r - 2, 2 * r - 1):
                            ins = dve.tensor_scalar(xn[:, t, :], res[:, t, :], mv[:, t, 0:1], rstd[:, t:t + 1],
                                                    ALU.subtract, ALU.mult)
                        ins.then_inc(s_xn, 1)

            def turns(n):
                for r in range(NP_):
                    dve.wait_ge(s_thi, NP_ * n + r + 1)
                    src = bank[r % 2][:].rearrange("p (k t) -> p k t", k=KT)
                    at = (slice(None), slice(None), slice(2 * P * r, 2 * P * (r + 1)))
                    dve.tensor_tensor(xnT[1][at], src, xnT[0][at].bitcast(F32), ALU.subtract).then_inc(s_tlo, 1)

            def over_e(a):
                return a.unsqueeze(2).to_broadcast([P, NT, E])

            def over_t(a):
                return a[:, None, :].to_broadcast([P, NT, E])

            def route(f):
                dve.wait_ge(s_rt, f + 1)
                if f == 0:
                    dve.wait_ge(s_small, 80)
                    dve.wait_ge(s_const, 2)
                tt, red = dve.tensor_tensor, dve.tensor_reduce
                link(tt(lg[:], bank[2][:, 0:NT * E].rearrange("p (t e) -> p t e", e=E), over_t(rb[:]), ALU.add))
                link(red(mx[:], lg[:], AX.X, ALU.max))
                tt(lg[:], lg[:], over_e(mx[:]), ALU.subtract).then_inc(s_lg, 1)
                dve.wait_ge(s_ex, f + 1)
                link(red(mx[:], pr[:], AX.X, ALU.add))
                link(dve.reciprocal(rsum[:], mx[:]))
                link(tt(pr[:], pr[:], over_e(rsum[:]), ALU.mult))
                for k in range(2):
                    src = pr
                    if k:
                        link(dve.scalar_tensor_tensor(out=lg[:].rearrange("p t e -> p (t e)"),
                                                      in0=oh[:, 0].rearrange("p t e -> p (t e)"), scalar=-4.0,
                                                      in1=pr[:].rearrange("p t e -> p (t e)"), op0=ALU.mult,
                                                      op1=ALU.add))
                        src = lg
                    link(red(top[:, k, :], src[:], AX.X, ALU.max))
                    link(tt(tmp[:], src[:], over_e(top[:, k, :]), ALU.is_equal))
                    link(tt(tmp[:], tmp[:], over_t(dn[:]), ALU.mult))
                    link(red(fst[:], tmp[:], AX.X, ALU.max))
                    link(tt(oh[:, k], over_t(dn[:]), over_e(fst[:]), ALU.is_equal))
                tt(ohs[:], oh[:, 0], oh[:, 1], ALU.add).then_inc(s_oh, 1)
                link(tt(fst[:], top[:, 0, :], top[:, 1, :], ALU.add))
                link(dve.tensor_scalar(fst[:], fst[:], EPS_TOP, None, ALU.add))
                link(dve.reciprocal(rsum[:], fst[:]))
                link(dve.scalar_tensor_tensor(out=gate[:], in0=top[:], scalar=0.5,
                                              in1=rsum[:, None, :].to_broadcast([P, 2, NT]),
                                              op0=ALU.mult, op1=ALU.mult))
                dve.wait_ge(s_rk, f + 1)
                cnt = big[:, 0:E * NT].rearrange("p (e k) -> p e k", k=NT)
                link(tt(cnt, bank[4][:, 0:E].unsqueeze(2).to_broadcast([P, E, NT]),
                        kk[:, None, :].to_broadcast([P, E, NT]), ALU.is_gt))
                link(red(nblk[:], cnt, AX.X, ALU.add))
                before = big[:, 0:E * E].rearrange("p (e g) -> p e g", g=E)
                link(tt(before, nblk[:, None, :].to_broadcast([P, E, E]), lt[:], ALU.mult))
                link(red(base[:], before, AX.X, ALU.add))
                link(dve.tensor_scalar(nblk[:], base[:], float(P), None, ALU.mult))
                link(tt(tmp[:], bank[3][:, 0:NT * E].rearrange("p (t e) -> p t e", e=E), over_t(nblk[:]), ALU.add))
                for k in range(2):
                    link(tt(oh[:, k], oh[:, k], tmp[:], ALU.mult))
                with nc.allow_low_precision(reason="sums of whole numbers, exact in float32"):
                    link(red(slot[:], oh[:], AX.X, ALU.add))
                link(tt(incl[0:1, 0:E - 1], base[0:1, 1:E], base[0:1, 1:E], ALU.max))
                ends = big[0:1, 0:NB * (E - 1)].rearrange("p (b e) -> p b e", e=E - 1)
                link(tt(ends, incl[:, None, 0:E - 1].to_broadcast([1, NB, E - 1]),
                        bno[:].unsqueeze(2).to_broadcast([1, NB, E - 1]), ALU.is_le))
                with nc.allow_low_precision(reason="sums of whole numbers, exact in float32"):
                    link(red(bex[:], ends, AX.X, ALU.add))
                dve.tensor_scalar(bexi[:, 0:NB], bex[:], float(WE), None, ALU.mult).then_inc(s_slot, 1)

            def hidden(j, par):
                dve.wait_ge(s_sg, j + 1)

            def times_up(j, par, first):
                dve.wait_ge(s_sg, j + 1)
                if not first:
                    dve.wait_ge(s_ht, j - 1)
                dve.tensor_tensor(hm[par][:], sg[par][:], bank[2 + par][:, F:GU], ALU.mult).then_inc(s_hm, 1)

            def hidden_low(j, par):
                dve.wait_ge(s_hth, j + 1)
                dve.tensor_tensor(hT[par][1][:], bank[4 + par][:, 0:P], hT[par][0][:].bitcast(F32), ALU.subtract)\
                    .then_inc(s_htl, 1)

            def ffn(f):
                route(f)
                for i in range(NT + 3):
                    j = f * NJ + i
                    if i < NT:
                        times_up(j, j % 2, f == 0 and i < 2)
                    if 0 <= i - 1 < NT:
                        hidden_low(j - 1, (j - 1) % 2)
                    if 0 <= i - 3 < NT:
                        dve.wait_ge(s_y, j - 2)
                        dve.scalar_tensor_tensor(out=res[:, i - 3, :], in0=bank[6 + (j - 3) % 2][:, 0:D], scalar=0.5,
                                                 in1=res[:, i - 3, :], op0=ALU.mult, op1=ALU.add).then_inc(s_ysh, 1)
                if f == 0:
                    for q in range(POOL_PREPS, E + 1):
                        split_low(q)

                def step(b, live):
                    j = f * NJ + NT + b
                    if live[0]:
                        dve.wait_ge(s_xth, f * NB + b + 1)
                        dve.tensor_tensor(xT[b % 2][1][:], bank[b % 2][:, 0:D].rearrange("p (k t) -> p k t", k=KT),
                                          xT[b % 2][0][:].bitcast(F32), ALU.subtract).then_inc(s_xtl, 1)
                    if live[1]:
                        times_up(j - 1, (j - 1) % 2, b - 1 >= 2)
                    if live[2]:
                        hidden_low(j - 2, j % 2)
                    if live[3]:
                        r = (b - 3) % RING
                        dve.wait_ge(s_y, j - 2)
                        if f or b - 3 >= RING:
                            dve.wait_ge(s_ys[r], 16 * ((NB - r + RING - 1) // RING * f + (b - 3) // RING))
                        dve.tensor_copy(ysb[r][:], bank[6 + (j - 3) % 2][:, 0:D]).then_inc(s_ye, 1)

                over_blocks(step)
                dve.wait_ge(s_ysh, NT * (f + 1))
                for t in range(NT):
                    dve.wait_ge(s_yg[t % 4], 32 * (2 * f + t // 4 + 1))
                    link(dve.scalar_tensor_tensor(out=res[:, t, :], in0=yg[t % 4][:, 0, :], scalar=gate[:, 0, t:t + 1],
                                                  in1=res[:, t, :], op0=ALU.mult, op1=ALU.add))
                    dve.scalar_tensor_tensor(out=res[:, t, :], in0=yg[t % 4][:, 1, :], scalar=gate[:, 1, t:t + 1],
                                             in1=res[:, t, :], op0=ALU.mult, op1=ALU.add).then_inc(s_cmb, 1)

            norm(0, lambda r: dve.wait_ge(s_x[r], 16))
            dve.wait_ge(s_rw, 1)
            dve.tensor_tensor(rw[1][:], rw_s[:], rw[0][:].bitcast(F32), ALU.subtract).then_inc(s_rw, 1)
            turns(0)
            ffn(0)

            norm(1, lambda r: dve.wait_ge(s_cmb, 2 * r + 2))
            turns(1)
            for it in range(8):
                dve.wait_ge(s_ph, it + 1)
                if it >= 2:
                    dve.wait_ge(s_pl, it - 1)
                    dve.wait_ge(s_pd[it - 2], 48)
                link(dve.tensor_tensor(pq[it % 2][:], pf[it % 2][:], part[it % 2][0][:], ALU.subtract))
                dve.tensor_copy(part[it % 2][1][:], pq[it % 2][:]).then_inc(s_pm, 1)
            dve.wait_ge(s_vone, 1)
            for t in range(NT):
                dve.wait_ge(s_vp, t + 1)
                to = V[:, t, 0:H * VW].rearrange("p (h w) -> p h w", w=VW)[:, :, 0:HD]
                dve.tensor_tensor(to, bank[4 + t % 2][:, 0:D].rearrange("p (h w) -> p h w", w=HD),
                                  vb[:].rearrange("p (h w) -> p h w", w=HD), ALU.add).then_inc(s_v, 1)

            def maximum(n, i):
                g, num = n // G, QT * n + QT - 1 - i
                dve.wait_ge(s_s, num + 1)
                w = (i + 1) * P
                dve.tensor_tensor_reduce(junk[num % 2][:, 0:w], bank[num % 2][:, 0:w], dec[:, 512 - w:512], 1.0, NEG,
                                         ALU.add, ALU.max, mmax[g % 2][:, n % G * QT + i:n % G * QT + i + 1])\
                    .then_inc(s_max, 1)

            def normalise(g):
                c, hg = g // 4, g % 4
                dve.wait_ge(s_otr, g + 1)
                src = bank[7][:].rearrange("p (i u w) -> p i u w", i=QT, w=32)
                link(dve.reciprocal(rc[:], src[:, :, :, HD]))
                to = att[:, c * QT:(c + 1) * QT, hg * G * HD:(hg + 1) * G * HD].rearrange("p i (u w) -> p i u w", w=HD)
                dve.tensor_tensor(to, src[:, :, :, 0:HD], rc[:].unsqueeze(3).to_broadcast([P, QT, G, HD]), ALU.mult)\
                    .then_inc(s_att, 1)

            dve.wait_ge(s_pd[7], 48)
            dve.wait_ge(s_pd[6], 48)
            dve.wait_ge(s_const, 3)
            for n in range(-LEAD, NH + G + 1):
                ahead = n + LEAD
                if 0 <= ahead < NH:
                    for i in range(QT):
                        maximum(ahead, QT - 1 - i)
                if ahead % G == 0 and G <= ahead <= NH:
                    g = ahead // G - 1
                    dve.wait_ge(s_mt, g + 1)
                    if g >= 2:
                        dve.wait_ge(s_mr[g % 2], 32 * (g // 2))
                    dve.tensor_copy(mT[g % 2][:], bank[5][:].bitcast(BF16)[0:2 * G * QT, 0:P]).then_inc(s_mts, 1)
                if ahead % G == G - 1 and ahead < NH:
                    g = ahead // G
                    if g >= 2:
                        dve.wait_ge(s_mt, g - 1)
                    dve.wait_ge(s_max, QT * (ahead + 1))
                    link(dve.tensor_scalar(negm[g % 2][:, 0, :], mmax[g % 2][:], -1.0, None, ALU.mult))
                    dve.scalar_tensor_tensor(out=negm[g % 2][:, 1, :], in0=mmax[g % 2][:], scalar=-1.0,
                                             in1=negm[g % 2][:, 0, :], op0=ALU.mult, op1=ALU.subtract)\
                        .then_inc(s_nm, 1)
                if n % G == 0 and n >= 2 * G:
                    normalise(n // G - 2)
            turns(2)
            dve.wait_ge(s_resb, NT)
            for t in range(NT):
                dve.wait_ge(s_o, t + 1)
                dve.tensor_tensor(res[:, t, :], bank[2 + t % 2][:, 0:D], res[:, t, :], ALU.add).then_inc(s_res2, 1)
            norm(2, lambda r: dve.wait_ge(s_res2, 2 * r + 2))
            turns(3)
            ffn(1)


_INS = ["x", "q_w", "k_w", "v_w", "o_w", "qk_b", "v_b", "o_b", "r_w", "r_b", "experts"]


def _by_partition(a):
    return a.reshape(-1, P, a.shape[1]).transpose(1, 0, 2)


def kernel(**inputs):
    import numpy as np
    import concourse.bacc as bacc
    from concourse.bass_utils import run_bass_kernel_spmd

    a = {name.removeprefix("L0_"): np.asarray(v) for name, v in inputs.items()}
    given = {"x": a["attn_x"], "v_b": a["attn_v_b"], "o_b": a["attn_o_b"], "r_b": a["ffn_bias"]}
    for i in "qkvo":
        given[f"{i}_w"] = _by_partition(a[f"attn_{i}_w"].T)
    given["r_w"] = _by_partition(a["ffn_Wr"].T)
    given["qk_b"] = np.stack([a["attn_q_b"].reshape(-1, P), a["attn_k_b"].reshape(-1, P)]).transpose(2, 0, 1)
    g, u, d = (np.concatenate([a[f"ffn_W{i}"], a[f"ffn_sW{i}"][None]]) for i in "gud")
    n = len(g)
    gu = np.stack([w.reshape(n, -1, P, w.shape[2]) for w in (g, u)], axis=3)
    gu = gu.transpose(0, 2, 1, 3, 4).reshape(n, P, -1)
    given["experts"] = np.concatenate([gu, d], axis=2)
    nc = bacc.Bacc("TRN2", target_bir_lowering=False, num_devices=1)
    arrays, args = {}, []
    for name in _INS:
        arrays[f"in_{name}"] = v = np.ascontiguousarray(given[name])
        args.append(nc.dram_tensor(f"in_{name}", v.shape, mybir.dt.from_np(v.dtype), kind="ExternalInput").ap())
    args.append(nc.dram_tensor("out", given["x"].shape, F32, kind="ExternalOutput").ap())
    macaron_kernel(nc, *args)
    r = run_bass_kernel_spmd(nc, [arrays], core_ids=[0])
    return r.results[0]["out"]
```

```python
from contextlib import ExitStack

import concourse.bass as bass
from concourse import mybir

ALU = mybir.AluOpType
ACT = mybir.ActivationFunctionType
AX = mybir.AxisListType
F32 = mybir.dt.float32
F32R = mybir.dt.float32r
BF16 = mybir.dt.bfloat16
F16 = mybir.dt.float16
I32 = mybir.dt.int32
U32 = mybir.dt.uint32

P = 128
NEG = -3.0e38


def macaron_kernel(nc, x, q_w, k_w, v_w, o_w, qk_b, v_b, o_b, r_w, r_b, experts, out):
    B, SEQ, D = x.shape
    E = experts.shape[0] - 1
    F = experts.shape[2] // 6
    N = B * SEQ
    NT = N // P
    KT = D // P
    NP_ = NT // 2
    H, HD = 16, 16
    QT = SEQ // P
    NB = (2 * N + E * (P - 1)) // P
    G = 4
    NG = B * H // G
    RING = 4
    PEEL = 5
    EPS_LN, EPS_TOP = 1e-5, 1e-9
    WE = KT * 2 * F + D
    GU = 2 * F
    STK = 6 * HD
    STM = STK + 2
    STD = STM + 3
    VW = HD + 1
    assert (P, KT, F, NB, QT) == (128, 2, 128, 31, 4)

    x_v = x.rearrange("b (t p) d -> p (b t) d", p=P)
    out_v = out.rearrange("b (t p) d -> p (b t) d", p=P)
    slots_x = nc.dram_tensor("slots_x", (NB * P, D), F32, kind="Internal").ap()
    rows_d = nc.dram_tensor("rows_d", (5, SEQ), BF16, kind="Internal").ap()
    slots_y = nc.dram_tensor("slots_y", (NB * P, D), F32, kind="Internal").ap()
    parts_d = nc.dram_tensor("parts_d", (2, KT, B, 3, P, SEQ), BF16, kind="Internal").ap()

    with ExitStack() as ctx:
        def sb(name, shape, dt=F32, to=ctx):
            return to.enter_context(nc.sbuf_tensor(name, shape, dt))

        def sem(name):
            return ctx.enter_context(nc.semaphore(name))

        bank = [ctx.enter_context(nc.psum_tensor(f"bank{i}", [P, 512], F32)) for i in range(8)]

        wh = sb("wh", [P, E + 1, WE], F32R)
        r0 = ExitStack()
        w_raw = sb("w_raw", [P, E + 1, WE], F32, r0)
        r0.close()
        wl = sb("wl", [P, E + 1, WE], F32R)
        rw = [sb(f"rw_{i}", [P, KT, E], F32R) for i in "hl"]
        rw_s = sb("rw_s", [P, KT, E])
        res = sb("res", [P, NT, D])
        xn = sb("xn", [P, NT, D])
        att = xn
        ident = sb("ident", [P, P])
        ident_b = sb("ident_b", [P, P], BF16)
        ones_b = sb("ones_b", [P, P], BF16)
        below_b = sb("below_b", [P, P], BF16)
        stats = sb("stats", [P, NT, 6])
        mv = sb("mv", [P, NT, 2])
        rstd = sb("rstd", [P, NT])
        dev = sb("dev", [P, NT])
        warm = sb("warm", [P, 1])
        eps = sb("eps", [P, 1])
        dec = sb("dec", [P, 512])
        dec_d = sb("dec_d", [P, P], BF16)
        dec_b = sb("dec_b", [P, 1])
        qkb = sb("qkb", [P, 2, KT])
        vb = sb("vb", [P, D])
        ob = sb("ob", [P, D])
        rb = sb("rb", [P, E])
        dn = sb("dn", [P, E])
        kk = sb("kk", [P, NT])
        lt = sb("lt", [P, E, E], BF16)
        bno = sb("bno", [1, NB])
        mx = sb("mx", [P, NT])
        rsum = sb("rsum", [P, NT])
        top = sb("top", [P, 2, NT])
        fst = sb("fst", [P, NT])
        gate = sb("gate", [P, 2, NT])
        nblk = sb("nblk", [P, E])
        base = sb("base", [P, E])
        incl = sb("incl", [1, E])
        bex = sb("bex", [1, NB])
        bexi = sb("bexi", [1, NB + 1], I32)
        slot = sb("slot", [P, 2, NT], U32)

        r1 = ExitStack()
        xnT = [sb(f"xnT_{i}", [P, KT, N], F32R, r1) for i in "hl"]
        r1.close()
        r1 = ExitStack()
        sb("below_wa", [P, 2 * KT * N], F32, r1)
        r0 = ExitStack()
        wa_raw = [sb(f"wa_raw{j}", [P, KT, D], F32, r0) for j in "qkv"]
        r0.close()
        wa_l = [sb(f"wa{j}_l", [P, KT, D], F32R, r1) for j in "qkv"]
        wa = [[sb(f"wa{j}_h", [P, KT, D], F32R, r1), wa_l[j]] for j in range(3)]
        r1.close()
        ct = [sb(f"ct{i}", [P, 1280]) for i in range(6)]
        r2 = ExitStack()
        yg = [sb(f"yg{i}", [P, 2, D], F32, r2) for i in range(4)]
        xb = [sb(f"xb{i}", [P, D], F32, r2) for i in range(RING)]
        xT = [[sb(f"xT{j}_{i}", [P, KT, P], F32R, r2) for i in "hl"] for j in range(2)]
        sg = [sb(f"sg{i}", [P, F], F32, r2) for i in range(2)]
        hm = [sb(f"hm{i}", [P, F], F32, r2) for i in range(2)]
        hT = [[sb(f"hT{j}_{i}", [P, P], F32R, r2) for i in "hl"] for j in range(2)]
        ysb = [sb(f"ysb{i}", [P, D], F32, r2) for i in range(RING)]
        zeros = sb("zeros", [P, D], F32, r2)
        lgT = sb("lgT", [E, N], F32, r2)
        lg = sb("lg", [P, NT, E], F32, r2)
        pr = sb("pr", [P, NT, E], F32, r2)
        tmp = sb("tmp", [P, NT, E], F32, r2)
        oh = sb("oh", [P, 2, NT, E], F32, r2)
        ohs = sb("ohs", [P, NT, E], BF16, r2)
        big = sb("big", [P, NB * E], F32, r2)
        iota_i = sb("iota_i", [P, 512], I32, r2)
        rows = sb("rows", [1, 5, SEQ], BF16, r2)
        r2.close()
        stk_k = [sb(f"stk_k{i}", [STD, G, SEQ], BF16) for i in range(3)]
        stk_q = [sb(f"stk_q{i}", [STD, G, SEQ], BF16) for i in range(3)]
        r3 = ExitStack()
        pq = [sb(f"pq{i}", [P, 512], F32, r3) for i in range(2)]
        part = [sb(f"part{j}", [P, 3, SEQ], BF16, r3) for j in range(3)]
        for t in (0, NT // 2):
            part.append(xn[:, t:t + 3, :].rearrange("p t d -> p (t d)").bitcast(BF16)
                        .rearrange("p (i t) -> p i t", i=3))
        r3.close()
        r3 = ExitStack()
        junk = [sb(f"junk{i}", [P, 512], BF16, r3) for i in range(3)]
        negm = [sb(f"negm{i}", [P, 2, G * QT], BF16, r3) for i in range(2)]
        mmax = [sb(f"mmax{i}", [P, G * QT], F32, r3) for i in range(2)]
        mT = [sb(f"mT{i}", [2 * G * QT, P], BF16, r3) for i in range(2)]
        rc = sb("rc", [P, QT, G], F32, r3)
        osb = [sb(f"osb{i}", [P, 512], F32, r3) for i in range(2)]
        wo_h = sb("wo_h", [P, KT, D], F32R, r3)
        r0 = ExitStack()
        wo_raw = sb("wo_raw", [P, KT, D], F32, r0)
        r0.close()
        wo = [wo_h, sb("wo_l", [P, KT, D], F32R, r3)]
        r3.close()
        sb("below_v", [P, 3584], F32)
        V = sb("V", [P, NT, H * VW + 16])

        s_x = [sem(f"s_x{r}") for r in range(NP_)]
        s_small = sem("s_small")
        s_const = sem("s_const")
        s_w = [sem(f"s_w{q}") for q in range(E + 1)]
        s_whi = sem("s_whi")
        s_wlo_p = sem("s_wlo_p")
        s_wlo_v = sem("s_wlo_v")
        s_rw = sem("s_rw")
        s_zero = sem("s_zero")
        s_fill = sem("s_fill")
        s_dv = sem("s_dv")
        s_pool = sem("s_pool")
        s_mv = sem("s_mv")
        s_dev = sem("s_dev")
        s_xn = sem("s_xn")
        s_tr = sem("s_tr")
        s_thi = sem("s_thi")
        s_tlo = sem("s_tlo")
        s_rt = sem("s_rt")
        s_lt = sem("s_lt")
        s_lr = sem("s_lr")
        s_lg = sem("s_lg")
        s_ex = sem("s_ex")
        s_oh = sem("s_oh")
        s_rk = sem("s_rk")
        s_slot = sem("s_slot")
        s_sc = sem("s_sc")
        s_xb = [sem(f"s_xb{i}") for i in range(RING)]
        s_xt = sem("s_xt")
        s_xth = sem("s_xth")
        s_xtl = sem("s_xtl")
        s_gu = sem("s_gu")
        s_sg = sem("s_sg")
        s_hm = sem("s_hm")
        s_ht = sem("s_ht")
        s_hth = sem("s_hth")
        s_htl = sem("s_htl")
        s_y = sem("s_y")
        s_ysh = sem("s_ysh")
        s_ye = sem("s_ye")
        s_ys = [sem(f"s_ys{i}") for i in range(RING)]
        s_yg = [sem(f"s_yg{i}") for i in range(4)]
        s_cmb = sem("s_cmb")
        s_was = [sem(f"s_was{i}") for i in range(3)]
        s_wap = sem("s_wap")
        s_qkb = sem("s_qkb")
        s_vone = sem("s_vone")
        s_ones = sem("s_ones")
        s_row = sem("s_row")
        s_dec = sem("s_dec")
        s_resb = sem("s_resb")
        s_qk = sem("s_qk")
        s_ph = sem("s_ph")
        s_pr = sem("s_pr")
        s_pm = sem("s_pm")
        s_pl = sem("s_pl")
        s_pd = [sem(f"s_pd{i}") for i in range(8)]
        s_vp = sem("s_vp")
        s_v = sem("s_v")
        s_stk = [sem(f"s_stk{i}") for i in range(3)]
        s_s = sem("s_s")
        s_max = sem("s_max")
        s_nm = sem("s_nm")
        s_mt = sem("s_mt")
        s_mts = sem("s_mts")
        s_mr = [sem(f"s_mr{i}") for i in range(2)]
        s_st = sem("s_st")
        s_exp = sem("s_exp")
        s_pv = sem("s_pv")
        s_ot = sem("s_ot")
        s_otr = sem("s_otr")
        s_att = sem("s_att")
        s_wos = sem("s_wos")
        s_wo = sem("s_wo")
        s_o = sem("s_o")
        s_res2 = sem("s_res2")
        s_out = sem("s_out")

        order = [E] + list(range(E))
        POOL_LOWS = range(2, 8)
        VEC_LOWS = [q for q in range(E + 1) if q not in POOL_LOWS]
        NJ = NT + NB
        behind = {0: (3, 0), 2: (3, 384), 1: (4, 0)}
        off = [512, 1024, 896]
        LEAD = 6
        s_bank = [0, 1, 5]
        NH = B * H
        NS_CONST = 19

        def three(eng, to, xs, ws, ins):
            terms = [(k, a, b) for k in range(KT) for a, b in ((0, 0), (0, 1), (1, 0))] if ins is None else ins
            for i, (k, a, b) in enumerate(terms):
                mm = eng.matmul(to, xs(k, a), ws(k, b), start=i == 0, stop=i == len(terms) - 1)
            return mm

        def back(q, r, k):
            return q + (r - k) // RING, (r - k) % RING

        def over_blocks(step):
            for b in range(NB + 3):
                step(b, [0 <= b - k < NB for k in range(4)])

        block = ctx.enter_context(nc.Block())

        @block.sync
        def _(sp):
            def load_x(r):
                sp.dma_start(res[:, 2 * r:2 * r + 2, :], x_v[:, 2 * r:2 * r + 2, :]).then_inc(s_x[r], 16)

            def load_expert(q):
                sp.dma_start(w_raw[:, order[q], :], experts[order[q]]).then_inc(s_w[q], 16)

            for r in range(NP_):
                load_x(r)
            sp.dma_start(rw_s[:], r_w).then_inc(s_small, 16)
            sp.dma_start(rb[:], r_b.partition_broadcast(P)).then_inc(s_small, 16)
            sp.dma_start(qkb[:], qk_b).then_inc(s_small, 16)
            sp.dma_start(vb[:], v_b.partition_broadcast(P)).then_inc(s_small, 16)
            sp.dma_start(ob[:], o_b.partition_broadcast(P)).then_inc(s_small, 16)
            for q in range(6):
                load_expert(q)
            sp.wait_ge(s_zero, 2)
            sp.dma_start(slots_x.rearrange("(p a) d -> p a d", p=P),
                         zeros[:, None, :].to_broadcast([P, NB, D])).then_inc(s_fill, 16)
            for q in range(6, E + 1):
                load_expert(q)
            sp.wait_ge(s_tlo, NP_)
            for j, w in enumerate((q_w, k_w, v_w)):
                sp.dma_start(wa_raw[j][:], w).then_inc(s_was[j], 16)

            def blocks(f):
                def load(q, r):
                    sp.dma_start(xb[r][:], slots_x[bass.ds((q * RING + r) * P, P), :]).then_inc(s_xb[r], 16)

                def step(q, r, live):
                    if live[0]:
                        sp.wait_ge(s_xt, q * RING + (r + f * NB + 1))
                        if not isinstance(q, int) or q * RING + r + RING < NB:
                            load(q + 1, r)
                    if live[3]:
                        q3, r3 = back(q, r, 3)
                        sp.wait_ge(s_ye, q3 * RING + (r3 + f * NB + 1))
                        sp.dma_start(slots_y[bass.ds((q3 * RING + r3) * P, P), :], ysb[r3][:]).then_inc(s_ys[r3], 16)

                sp.wait_ge(s_sc, 16 * 2 * NT * (f + 1))
                for b in range(RING):
                    load(0, b)
                turns_ = (NB - PEEL - RING) // RING
                for i in range(PEEL):
                    step(0 + i // RING, i % RING, [0 <= i - k for k in range(4)])
                with sp.Fori(0, turns_) as n:
                    for i in range(PEEL, PEEL + RING):
                        step(n + i // RING, i % RING, [True] * 4)
                for i in range(PEEL + turns_ * RING, NB + 3):
                    step(i // RING, i % RING, [0 <= i - k < NB for k in range(4)])

            def attention():
                def store_parts(it):
                    sp.wait_ge(s_pl, it + 1)
                    c, m, op = it // 4, it // 2 % 2, it % 2
                    sp.dma_start(parts_d[op, m, c].rearrange("i p t -> p i t"), part[it % 5][:])\
                        .then_inc(s_pd[it], 16)

                def load_stacks(g):
                    c, hg = g // 4, g % 4
                    for it in (4 * c + hg // 2 * 2, 4 * c + hg // 2 * 2 + 1):
                        sp.wait_ge(s_pd[it], 16)
                    if g >= 3:
                        sp.wait_ge(s_st, 3 * G * (g - 2))
                    for op, stk in ((1, stk_k), (0, stk_q)):
                        row = 0
                        for a, n in ((0, 3), (1, 2), (2, 1)):
                            src = parts_d[op, hg // 2, c].rearrange("i (d h) t -> d i h t", d=HD)
                            src = src[:, :, hg % 2 * G:(hg % 2 + 1) * G, :].rearrange("d i h t -> d i (h t)")
                            src = src[:, a:a + 1, :].to_broadcast([HD, n, G * SEQ]) if op else src[:, 0:n, :]
                            dst = stk[g % 3][row:row + n * HD, :, :].rearrange("p h t -> p (h t)")
                            sp.dma_start(dst, src).then_inc(s_stk[g % 3], 16)
                            row += n * HD

                def decay_rows(i):
                    dup = rows_d[:, None, :].to_broadcast([5, G, SEQ])
                    sp.dma_start(stk_k[i][STM:STD, :, :], dup[0:3]).then_inc(s_dec, 16)
                    sp.dma_start(stk_q[i][STM + 1:STD, :, :], dup[3:5]).then_inc(s_dec, 16)

                def store_maxima(g):
                    sp.wait_ge(s_mts, g + 1)
                    dst = stk_k[g % 3][STK:STM, :, :].rearrange("a u (i t) -> a (u i) t", t=P)
                    sp.dma_start(dst, mT[g % 2][:]).then_inc(s_mr[g % 2], 16)

                for it in (0, 1):
                    store_parts(it)
                load_stacks(0)
                for it in (2, 3, 4):
                    store_parts(it)
                load_stacks(1)
                sp.wait_ge(s_row, 16)
                for i in range(3):
                    decay_rows(i)
                for it in (5, 6, 7):
                    store_parts(it)
                load_stacks(2)
                store_maxima(0)
                store_maxima(1)
                for g in range(3, NG):
                    load_stacks(g)
                    store_maxima(g - 1)
                store_maxima(NG - 1)

            blocks(0)
            attention()
            blocks(1)
            for t in range(NT):
                sp.wait_ge(s_cmb, NT + t + 1)
                sp.dma_start(out_v[:, t, :], res[:, t, :]).then_inc(s_out, 16)
            sp.wait_ge(s_out, 16 * NT)

        @block.gpsimd
        def _(pool):
            steps = [0]

            def link(ins):
                steps[0] += 1
                ins.then_inc(s_pool, 1)
                pool.wait_ge(s_pool, steps[0])

            pool.memset(eps[:], EPS_LN).then_inc(s_zero, 1)
            pool.memset(zeros[:], 0.0).then_inc(s_zero, 1)
            link(pool.memset(ident[:], 0.0))
            pool.affine_select(out=ident[:], in_=ident[:], compare_op=ALU.not_equal, fill=1.0, base=0,
                               pattern=[[-1, P]], channel_multiplier=1).then_inc(s_const, 1)

            link(pool.iota(iota_i[:, 0:E], pattern=[[-1, E]], base=E, channel_multiplier=0))
            link(pool.tensor_copy(dn[:], iota_i[:, 0:E]))
            link(pool.iota(iota_i[:, 0:NT], pattern=[[P, NT]], base=0, channel_multiplier=0))
            link(pool.tensor_copy(kk[:], iota_i[:, 0:NT]))
            link(pool.iota(iota_i[0:1, 0:NB], pattern=[[1, NB]], base=0, channel_multiplier=0))
            link(pool.tensor_copy(bno[:], iota_i[0:1, 0:NB]))
            link(pool.memset(lt[:], 1.0))
            link(pool.affine_select(out=lt[:], in_=lt[:], compare_op=ALU.is_gt, fill=0.0, base=0,
                                    pattern=[[1, E], [-1, E]], channel_multiplier=0))
            link(pool.memset(ones_b[:], 1.0))
            link(pool.affine_select(out=below_b[:], in_=ones_b[:], compare_op=ALU.is_gt, fill=0.0, base=0,
                                    pattern=[[1, P]], channel_multiplier=-1))
            pool.tensor_copy(ident_b[:], ident[:]).then_inc(s_const, 1)

            def split_low(q):
                e = order[q]
                pool.wait_ge(s_whi, q + 1)
                pool.tensor_tensor(wl[:, e, :], w_raw[:, e, :], wh[:, e, :].bitcast(F32), ALU.subtract)\
                    .then_inc(s_wlo_p, 1)

            for q in POOL_LOWS:
                split_low(q)

            def scatter(f):
                pool.wait_ge(s_slot, f + 1)
                if f == 0:
                    pool.wait_ge(s_fill, 16)
                for t in range(NT):
                    for k in range(2):
                        pool.indirect_dma_start(slots_x, bass.IndirectOffsetOnAxis(ap=slot[:, k, t:t + 1], axis=0),
                                                xn[:, t, :], None).then_inc(s_sc, 16)

            def gather(f):
                for r in range(RING):
                    uses = (NB - r + RING - 1) // RING
                    pool.wait_ge(s_ys[r], 16 * uses * (f + 1))
                for t in range(NT):
                    if t >= 4:
                        pool.wait_ge(s_cmb, NT * f + t - 3)
                    for k in range(2):
                        pool.indirect_dma_start(yg[t % 4][:, k, :], None, slots_y,
                                                bass.IndirectOffsetOnAxis(ap=slot[:, k, t:t + 1], axis=0))\
                            .then_inc(s_yg[t % 4], 16)

            scatter(0)
            pool.wait_ge(s_small, 80)
            pool.tensor_scalar(qkb[:, 0, :], qkb[:, 0, :], HD ** -0.5, None, ALU.mult).then_inc(s_qkb, 1)
            link(pool.iota(iota_i[:], pattern=[[1, 512]], base=-384, channel_multiplier=-1))
            link(pool.tensor_copy(dec[:], iota_i[:]))
            link(pool.affine_select(out=dec[:], in_=dec[:], compare_op=ALU.is_ge, fill=NEG, base=384,
                                    pattern=[[-1, 512]], channel_multiplier=1))
            link(pool.iota(iota_i[:, 0:P], pattern=[[-1, P]], base=0, channel_multiplier=1))
            link(pool.tensor_copy(dec_d[:], iota_i[:, 0:P]))
            link(pool.affine_select(out=dec_d[:], in_=dec_d[:], compare_op=ALU.is_ge, fill=NEG, base=0,
                                    pattern=[[1, P]], channel_multiplier=-1))
            link(pool.iota(iota_i[:, 0:1], pattern=[[1, 1]], base=1 - P, channel_multiplier=1))
            pool.tensor_copy(dec_b[:], iota_i[:, 0:1]).then_inc(s_const, 1)
            link(pool.memset(rows[:], 0.0))
            for k, lo, hi, value in ((1, 2, 3, -P), (1, 3, 4, -2 * P), (2, 3, 4, -P), (3, 0, 1, 1), (4, 1, 2, 1)):
                link(pool.memset(rows[:, k, lo * P:hi * P], float(value)))
            link(pool.iota(iota_i[0:1, :], pattern=[[0, QT], [-1, P]], base=-1, channel_multiplier=0))
            link(pool.tensor_copy(rows[:, 0, :], iota_i[0:1, :]))
            pool.dma_start(rows_d[None, :, :], rows[:]).then_inc(s_row, 16)
            pool.wait_ge(s_row, 16)
            pool.memset(V[:], 1.0).then_inc(s_vone, 1)
            for j in range(3):
                raw = wa_raw[j][:]
                pool.wait_ge(s_was[j], 16)
                if j == 0:
                    link(pool.tensor_scalar(raw, raw, HD ** -0.5, None, ALU.mult))
                link(pool.tensor_copy(wa[j][0][:], raw))
                link(pool.tensor_tensor(wa[j][1][:], raw, wa[j][0][:].bitcast(F32), ALU.subtract))
            pool.nop().then_inc(s_wap, 1)
            gather(0)

            for it in range(8):
                if it == 3:
                    pool.wait_ge(s_xn, 2 * NP_)
                    pool.wait_ge(s_pl, it)
                    for i in range(3):
                        pool.memset(stk_q[i][STK:STM + 1, :, :], 1.0).then_inc(s_ones, 1)
                    pool.wait_ge(s_ones, 3)
                pool.wait_ge(s_pm, it + 1)
                pool.tensor_tensor(part[it % 5][:, 2, :], pq[it % 2][:], part[it % 5][:, 1, :], ALU.subtract)\
                    .then_inc(s_pl, 1)
            for t in range(NT):
                pool.tensor_tensor(res[:, t, :], res[:, t, :], ob[:], ALU.add).then_inc(s_resb, 1)
            for it in range(3, 8):
                pool.wait_ge(s_pd[it], 16)
            raw = wo_raw[:]
            pool.dma_start(raw, o_w).then_inc(s_wos, 16)
            pool.wait_ge(s_wos, 16)
            link(pool.tensor_copy(wo[0][:], raw))
            pool.tensor_tensor(wo[1][:], raw, wo[0][:].bitcast(F32), ALU.subtract).then_inc(s_wo, 1)

            scatter(1)
            gather(1)

        @block.scalar
        def _(act):
            def load_table(func):
                act.activation(warm[:], eps[:], func)

            def split_high(q):
                act.wait_ge(s_w[q], 16)
                act.activation(wh[:, order[q], :], w_raw[:, order[q], :], ACT.Copy).then_inc(s_whi, 1)

            def deviation(n, r):
                act.wait_ge(s_mv, NP_ * n + r + 1)
                act.activation(dev[:, 2 * r:2 * r + 2], mv[:, 2 * r:2 * r + 2, 1], ACT.Sqrt, bias=eps[:])\
                    .then_inc(s_dev, 1)

            def turn_high(n, r):
                act.wait_ge(s_tr, NP_ * n + r + 1)
                src = bank[r % 2][:].rearrange("p (k t) -> p k t", k=KT)
                act.activation(xnT[0][:, :, 2 * P * r:2 * P * (r + 1)], src, ACT.Copy).then_inc(s_thi, 1)

            def norm_turns(n, turn):
                for r in range(NP_ + 2):
                    if r < NP_:
                        deviation(n, r)
                    if r >= 2:
                        turn_high(turn, r - 2)

            def hidden(j, par, first):
                act.wait_ge(s_gu, j + 1)
                if not first:
                    act.wait_ge(s_hm, j - 1)
                act.activation(sg[par][:], bank[2 + par][:, 0:F], ACT.Silu).then_inc(s_sg, 1)

            def hidden_high(j, par, first):
                act.wait_ge(s_ht, j + 1)
                if not first:
                    act.wait_ge(s_y, j - 1)
                act.activation(hT[par][0][:], bank[4 + par][:, 0:P], ACT.Copy).then_inc(s_hth, 1)

            def ffn(f):
                load_table(ACT.Exp)
                for i in range(2):
                    act.wait_ge(s_rt, 2 * f + i + 1)
                    act.activation(lgT[:, i * 512:(i + 1) * 512], bank[2 + i][0:E, :], ACT.Copy).then_inc(s_lt, 1)
                act.wait_ge(s_lg, f + 1)
                act.activation(pr[:], lg[:], ACT.Exp).then_inc(s_ex, 1)
                load_table(ACT.Silu)
                if f == 0:
                    for q in range(2, E + 1):
                        split_high(q)
                for i in range(NT + 2):
                    if i < NT:
                        hidden(f * NJ + i, (f * NJ + i) % 2, i < 2 and not f)
                    if 0 <= i - 1 < NT:
                        hidden_high(f * NJ + i - 1, (f * NJ + i - 1) % 2, i - 1 < 2 and not f)

                def step(b, live):
                    j = f * NJ + NT + b
                    if live[0]:
                        act.wait_ge(s_xt, f * NB + b + 1)
                        if b < 2:
                            act.wait_ge(s_gu, j - 1)
                        act.activation(xT[b % 2][0][:], bank[b % 2][:, 0:D].rearrange("p (k t) -> p k t", k=KT),
                                       ACT.Copy).then_inc(s_xth, 1)
                    if live[1]:
                        hidden(j - 1, (j - 1) % 2, False)
                    if live[2]:
                        hidden_high(j - 2, j % 2, False)

                over_blocks(step)

            act.wait_ge(s_zero, 2)
            load_table(ACT.Sqrt)
            norm_turns(0, 0)
            act.wait_ge(s_small, 80)
            act.activation(rw[0][:], rw_s[:], ACT.Copy).then_inc(s_rw, 1)
            for q in range(2):
                split_high(q)
            ffn(0)

            def part_high(it):
                m, op = it // 2 % 2, it % 2
                act.wait_ge(s_qk, it + 1)
                if it >= 5:
                    act.wait_ge(s_pd[it - 5], 16)
                act.activation(part[it % 5][:, 0, :], bank[2 + it % 2][:], ACT.Identity, bias=qkb[:, op, m:m + 1])\
                    .then_inc(s_ph, 1)

            load_table(ACT.Sqrt)
            act.wait_ge(s_qkb, 1)
            for r in range(3):
                deviation(1, r)
                if r < 2:
                    turn_high(1, r)
            for it in range(3):
                part_high(it)
            deviation(1, 3)
            part_high(3)
            for r in (2, 3):
                turn_high(1, r)
            for it in range(4, 8):
                part_high(it)
            load_table(ACT.Exp)

            def out_of_v(g):
                act.wait_ge(s_pv, g + 1)
                if g >= 2:
                    act.wait_ge(s_otr, g - 1)
                if g == 0:
                    for it in range(3, 8):
                        act.wait_ge(s_pd[it], 16)
                act.activation(osb[g % 2][:], bank[6][:], ACT.Copy).then_inc(s_ot, 1)

            for n in range(NH):
                for i, (a, b) in enumerate(((0, 512), (512, 1024), (1024, 1280))):
                    act.wait_ge(s_st, 3 * n + i + 1)
                    if n >= 6 and i == 0:
                        act.wait_ge(s_pv, (n - 6) // G + 1)
                    act.activation(ct[n % 6][:, a:b], bank[2 + i][:, 0:b - a], ACT.Exp, bias=dec_b[:] if i else 0.0)\
                        .then_inc(s_exp, 1)
                if n % G == 2 and n > G:
                    out_of_v(n // G - 1)
            out_of_v(NG - 1)
            for r in range(NP_):
                turn_high(2, r)
            load_table(ACT.Sqrt)
            norm_turns(2, 3)
            ffn(1)

        @block.tensor
        def _(pe):
            def turn(n, r):
                if r >= 2:
                    pe.wait_ge(s_tlo, NP_ * n + r - 1)
                for k in range(KT):
                    for t in range(2):
                        mm = pe.transpose(bank[r % 2][:, (2 * k + t) * P:(2 * k + t + 1) * P],
                                          xn[:, 2 * r + t, k * P:(k + 1) * P], ident[:])
                mm.then_inc(s_tr, 1)

            def rows(t):
                return lambda k, a: xnT[a][:, k, t * P:(t + 1) * P]

            def gate_up(j, par, first, xs, ws):
                if not first:
                    pe.wait_ge(s_hm, j - 1)
                three(pe, bank[2 + par][:, 0:GU], xs, ws, None).then_inc(s_gu, 1)

            def hidden_turn(j, par, first):
                pe.wait_ge(s_hm, j + 1)
                if not first:
                    pe.wait_ge(s_htl, j - 1)
                pe.transpose(bank[4 + par][:, 0:P], hm[par][:], ident[:]).then_inc(s_ht, 1)

            def down(j, par, wd):
                pe.wait_ge(s_htl, j + 1)
                three(pe, bank[6 + par][:, 0:D], lambda k, a: hT[par][a][:], lambda k, b: wd(b),
                      [(0, 0, 0), (0, 0, 1), (0, 1, 0)]).then_inc(s_y, 1)

            def ffn(f, n):
                for r in range(NP_):
                    pe.wait_ge(s_tlo, NP_ * n + r + 1)
                    mm = three(pe, bank[2 + r // 2][0:E, r % 2 * 2 * P:(r % 2 + 1) * 2 * P],
                               lambda k, a: rw[a][:, k, :],
                               lambda k, b: xnT[b][:, k, 2 * r * P:2 * (r + 1) * P], None)
                    if r % 2:
                        mm.then_inc(s_rt, 1)
                for t in range(NT):
                    if t % 4 == 0:
                        pe.wait_ge(s_lt, 2 * f + t // 4 + 1)
                    mm = pe.transpose(bank[6][:, t * E:(t + 1) * E], lgT[:, t * P:(t + 1) * P], ident[0:E, 0:E])
                mm.then_inc(s_lr, 1)
                pe.wait_ge(s_oh, f + 1)
                flat = ohs[:].rearrange("p t e -> p (t e)")
                pe.matmul(bank[3][:, 0:NT * E], below_b[:], flat, start=True, stop=False, skip_group_check=True)
                for s in range(1, NT):
                    pe.matmul(bank[3][:, s * E:NT * E], ones_b[:], flat[:, 0:(NT - s) * E], start=False,
                              stop=s == NT - 1, skip_group_check=True)
                for t in range(NT):
                    mm = pe.matmul(bank[4][:, 0:E], ones_b[:], flat[:, t * E:(t + 1) * E], start=t == 0,
                                   stop=t == NT - 1)
                mm.then_inc(s_rk, 1)
                if f == 0:
                    pe.wait_ge(s_wlo_v, 1)
                pe.wait_ge(s_slot, f + 1)

                def w_s(k, b):
                    return (wh, wl)[b][:, E, k * GU:(k + 1) * GU]

                for i in range(NT + 2):
                    j = f * NJ + i
                    if i < NT:
                        gate_up(j, j % 2, f == 0 and i < 2, rows(i), w_s)
                    if 0 <= i - 1 < NT:
                        hidden_turn(j - 1, (j - 1) % 2, f == 0 and i - 1 < 2)
                    if 0 <= i - 2 < NT:
                        if i - 2 >= 2:
                            pe.wait_ge(s_ysh, f * NT + i - 3)
                        down(j - 2, j % 2, lambda b: (wh, wl)[b][:, E, KT * GU:WE])
                pe.wait_ge(s_ysh, (f + 1) * NT)
                if f == 0:
                    pe.wait_ge(s_wlo_v, len(VEC_LOWS))
                    pe.wait_ge(s_wlo_p, len(POOL_LOWS))

                whl = [w[:].rearrange("p e n -> p (e n)") for w in (wh, wl)]
                at = {}

                def step(b, live):
                    j, n = f * NJ + NT + b, f * NB + b
                    if b % RING == 0 and b < NB:
                        regs = [pe.alloc_register(f"expert{f}_{i}") for i in range(b, min(b + RING, NB))]
                        pe.load(regs, bexi[0:1, b:b + len(regs)])
                        for i, reg in enumerate(regs):
                            at[b + i] = pe.snap(reg, donate=True, min_val=0, max_val=(E - 1) * WE)
                    if live[0]:
                        pe.wait_ge(s_xb[b % RING], 16 * (f * ((NB - b % RING + RING - 1) // RING) + b // RING + 1))
                        if b < 2 and f:
                            pe.wait_ge(s_xtl, n - 1)
                        for k in range(KT):
                            mm = pe.transpose(bank[b % 2][:, k * P:(k + 1) * P],
                                              xb[b % RING][:, k * P:(k + 1) * P], ident[:])
                        mm.then_inc(s_xt, 1)
                    if live[1]:
                        pe.wait_ge(s_xtl, n)
                        gate_up(j - 1, (j - 1) % 2, b - 1 >= 2, lambda k, a: xT[(b - 1) % 2][a][:, k, :],
                                lambda k, c: whl[c][:, bass.ds(at[b - 1] + k * GU, GU)])
                    if live[2]:
                        hidden_turn(j - 2, j % 2, b - 2 >= 2)
                    if live[3]:
                        if f or b >= 5:
                            pe.wait_ge(s_ye, n - 4)
                        down(j - 3, (j - 3) % 2, lambda c: whl[c][:, bass.ds(at[b - 3] + KT * GU, D)])

                over_blocks(step)

            pe.wait_ge(s_const, 1)
            for r in range(NP_):
                pe.wait_ge(s_xn, r + 1)
                turn(0, r)
            pe.wait_ge(s_rw, 2)
            pe.wait_ge(s_const, 2)
            ffn(0, 0)

            def v_products(c):
                for t in range(c * QT, (c + 1) * QT):
                    if t >= 2:
                        pe.wait_ge(s_v, t - 1)
                    three(pe, bank[4 + t % 2][:, 0:D], rows(t), lambda k, b: wa[2][b][:, k, :], None)\
                        .then_inc(s_vp, 1)

            def qk_product(it):
                c, m, op = it // 4, it // 2 % 2, it % 2
                if it >= 2:
                    pe.wait_ge(s_pr, it - 1)
                three(pe, bank[2 + it % 2][:], lambda k, a: wa[op][a][:, k, m * P:(m + 1) * P],
                      lambda k, b: xnT[b][:, k, c * SEQ:(c + 1) * SEQ], None).then_inc(s_qk, 1)

            for c in range(B):
                for r in (2 * c, 2 * c + 1):
                    pe.wait_ge(s_xn, NP_ + r + 1)
                    turn(1, r)
                if c == 0:
                    pe.wait_ge(s_wap, 1)
                else:
                    v_products(0)
                pe.wait_ge(s_tlo, NP_ + 2 * c + 2)
                for it in range(4 * c, 4 * c + 4):
                    qk_product(it)
            v_products(1)

            def score(n, i):
                g, u, num = n // G, n % G, QT * n + QT - 1 - i
                if n % G == 0 and i == QT - 1:
                    pe.wait_ge(s_stk[g % 3], 96 * (g // 3 + 1))
                if num >= 3:
                    pe.wait_ge(s_max, num - 2)
                pe.matmul(bank[s_bank[num % 3]][:, 0:(i + 1) * P], stk_k[g % 3][0:STK, u, i * P:(i + 1) * P],
                          stk_q[g % 3][0:STK, u, 0:(i + 1) * P], start=True, stop=True).then_inc(s_s, 1)

            def scores_t(n, i):
                g, u = n // G, n % G
                if n % G == 0 and i == 0:
                    pe.wait_ge(s_mr[g % 2], 16 * (g // 2 + 1))
                if n >= 1:
                    pe.wait_ge(s_exp, 3 * (n - 1) + i + 1)
                q, k = stk_q[g % 3], stk_k[g % 3]
                if i == 0:
                    pe.matmul(bank[2][:], ident_b[:], dec_d[:, None, :].to_broadcast([P, QT, P]), start=True,
                              stop=False, skip_group_check=True)
                    for j in range(QT):
                        tile = slice(j * P, (j + 1) * P)
                        mm = pe.matmul(bank[2][:, tile], q[0:STM, u, tile], k[0:STM, u, tile], start=False,
                                       stop=True, skip_group_check=True)
                else:
                    for j, (b, at) in behind.items():
                        if b == 2 + i:
                            mm = pe.matmul(bank[b][:, at:at + SEQ - (j + 1) * P], q[:, u, j * P:(j + 1) * P],
                                           k[:, u, (j + 1) * P:SEQ], start=True, stop=True)
                mm.then_inc(s_st, 1)

            def maxima_turn(g):
                pe.wait_ge(s_nm, g + 1)
                if g >= 3:
                    pe.wait_ge(s_att, g - 2)
                pe.transpose(bank[7][:].bitcast(BF16)[0:2 * G * QT, 0:P], negm[g % 2][:].rearrange("p a n -> p (a n)"),
                             ident_b[:]).then_inc(s_mt, 1)

            def times_v(g, j):
                c, hg = g // 4, g % 4
                if j == 0:
                    pe.wait_ge(s_exp, 3 * G * (g + 1))
                    if g >= 1:
                        pe.wait_ge(s_ot, g)
                for behind_it in (False, True)[0:1 + (j < QT - 1)]:
                    lo, hi, at = ((j + 1) * P, SEQ, off[j]) if behind_it else (j * P, (j + 1) * P, j * P)
                    for u in range(G):
                        n, h = G * g + u, G * hg + u
                        mm = pe.matmul(bank[6][32 * u:32 * u + 32, lo:hi], V[:, c * QT + j, h * VW:h * VW + 32],
                                       ct[n % 6][:, at:at + hi - lo], start=j == 0, stop=not behind_it,
                                       skip_group_check=True)
                if j == QT - 1:
                    mm.then_inc(s_pv, 1)

            def out_turn(g):
                pe.wait_ge(s_ot, g + 1)
                pe.wait_ge(s_mts, min(g + 3, NG))
                if g >= 1:
                    pe.wait_ge(s_att, g)
                for i in range(QT):
                    mm = pe.transpose(bank[7][:, i * P:(i + 1) * P], osb[g % 2][:, i * P:(i + 1) * P], ident[:])
                mm.then_inc(s_otr, 1)

            pe.wait_ge(s_pr, 8)
            pe.wait_ge(s_v, NT)
            pe.wait_ge(s_const, 3)
            for n in range(-LEAD, NH + G):
                ahead = n + LEAD
                if n == 0:
                    pe.wait_ge(s_ones, 3)
                    pe.wait_ge(s_dec, 96)
                for i in range(QT):
                    if 0 <= ahead < NH:
                        score(ahead, QT - 1 - i)
                    if 0 <= n < NH and i:
                        scores_t(n, i - 1)
                    if i == 1 and ahead % G == 0 and G <= ahead <= NH:
                        maxima_turn(ahead // G - 1)
                    if n >= G and n % G < 2 and i % 2:
                        times_v(n // G - 1, n % G * 2 + i // 2)
                if n % G == 3 and n > G:
                    out_turn(n // G - 1)

            for r in range(NP_):
                pe.wait_ge(s_att, 4 * (r // 2 + 1))
                turn(2, r)
            pe.wait_ge(s_tlo, 3 * NP_)
            pe.wait_ge(s_wo, 1)
            for t in range(NT):
                if t >= 2:
                    pe.wait_ge(s_res2, t - 1)
                three(pe, bank[2 + t % 2][:, 0:D], rows(t), lambda k, b: wo[b][:, k, :], None).then_inc(s_o, 1)
            for r in range(NP_):
                pe.wait_ge(s_xn, 2 * NP_ + r + 1)
                turn(3, r)
            ffn(1, 3)

        @block.vector
        def _(dve):
            steps = [0]

            def link(ins):
                steps[0] += 1
                ins.then_inc(s_dv, 1)
                dve.wait_ge(s_dv, steps[0])

            def split_low(i):
                q = VEC_LOWS[i]
                e = order[q]
                dve.wait_ge(s_whi, q + 1)
                dve.tensor_tensor(wl[:, e, :], w_raw[:, e, :], wh[:, e, :].bitcast(F32), ALU.subtract)\
                    .then_inc(s_wlo_v, 1)

            def statistics(r):
                for t in (2 * r, 2 * r + 1):
                    ins = dve.bn_stats(stats[:, t, :], res[:, t, :])
                link(ins)
                for t in (2 * r, 2 * r + 1):
                    ins = dve.bn_aggr(mv[:, t, :], stats[:, t, :])
                ins.then_inc(s_mv, 1)

            def normal_rows(n, r):
                dve.wait_ge(s_dev, NP_ * n + r + 1)
                link(dve.reciprocal(rstd[:, 2 * r:2 * r + 2], dev[:, 2 * r:2 * r + 2]))
                for t in (2 * r, 2 * r + 1):
                    ins = dve.tensor_scalar(xn[:, t, :], res[:, t, :], mv[:, t, 0:1], rstd[:, t:t + 1],
                                            ALU.subtract, ALU.mult)
                ins.then_inc(s_xn, 1)

            def turn_low(n, r):
                dve.wait_ge(s_thi, NP_ * n + r + 1)
                src = bank[r % 2][:].rearrange("p (k t) -> p k t", k=KT)
                at = (slice(None), slice(None), slice(2 * P * r, 2 * P * (r + 1)))
                dve.tensor_tensor(xnT[1][at], src, xnT[0][at].bitcast(F32), ALU.subtract).then_inc(s_tlo, 1)

            def norm(n, turn, ready):
                for r in range(NP_ + 2):
                    if r < NP_:
                        ready(r)
                        statistics(r)
                    if 1 <= r <= NP_:
                        normal_rows(n, r - 1)
                    if r >= 2:
                        turn_low(turn, r - 2)

            def over_e(a):
                return a.unsqueeze(2).to_broadcast([P, NT, E])

            def over_t(a):
                return a[:, None, :].to_broadcast([P, NT, E])

            def route(f):
                dve.wait_ge(s_lr, f + 1)
                if f == 0:
                    dve.wait_ge(s_small, 80)
                    dve.wait_ge(s_const, 2)
                tt, red = dve.tensor_tensor, dve.tensor_reduce
                link(tt(lg[:], bank[6][:, 0:NT * E].rearrange("p (t e) -> p t e", e=E), over_t(rb[:]), ALU.add))
                link(red(mx[:], lg[:], AX.X, ALU.max))
                tt(lg[:], lg[:], over_e(mx[:]), ALU.subtract).then_inc(s_lg, 1)
                dve.wait_ge(s_ex, f + 1)
                link(red(mx[:], pr[:], AX.X, ALU.add))
                link(dve.reciprocal(rsum[:], mx[:]))
                link(tt(pr[:], pr[:], over_e(rsum[:]), ALU.mult))
                for k in range(2):
                    src = pr
                    if k:
                        link(dve.scalar_tensor_tensor(out=lg[:].rearrange("p t e -> p (t e)"),
                                                      in0=oh[:, 0].rearrange("p t e -> p (t e)"), scalar=-4.0,
                                                      in1=pr[:].rearrange("p t e -> p (t e)"), op0=ALU.mult,
                                                      op1=ALU.add))
                        src = lg
                    link(red(top[:, k, :], src[:], AX.X, ALU.max))
                    link(tt(tmp[:], src[:], over_e(top[:, k, :]), ALU.is_equal))
                    link(tt(tmp[:], tmp[:], over_t(dn[:]), ALU.mult))
                    link(red(fst[:], tmp[:], AX.X, ALU.max))
                    link(tt(oh[:, k], over_t(dn[:]), over_e(fst[:]), ALU.is_equal))
                tt(ohs[:], oh[:, 0], oh[:, 1], ALU.add).then_inc(s_oh, 1)
                link(tt(fst[:], top[:, 0, :], top[:, 1, :], ALU.add))
                link(dve.tensor_scalar(fst[:], fst[:], EPS_TOP, None, ALU.add))
                link(dve.reciprocal(rsum[:], fst[:]))
                link(dve.scalar_tensor_tensor(out=gate[:], in0=top[:], scalar=0.5,
                                              in1=rsum[:, None, :].to_broadcast([P, 2, NT]),
                                              op0=ALU.mult, op1=ALU.mult))
                dve.wait_ge(s_rk, f + 1)
                cnt = big[:, 0:E * NT].rearrange("p (e k) -> p e k", k=NT)
                link(tt(cnt, bank[4][:, 0:E].unsqueeze(2).to_broadcast([P, E, NT]),
                        kk[:, None, :].to_broadcast([P, E, NT]), ALU.is_gt))
                link(red(nblk[:], cnt, AX.X, ALU.add))
                before = big[:, 0:E * E].rearrange("p (e g) -> p e g", g=E)
                link(tt(before, nblk[:, None, :].to_broadcast([P, E, E]), lt[:], ALU.mult))
                link(red(base[:], before, AX.X, ALU.add))
                link(dve.tensor_scalar(nblk[:], base[:], float(P), None, ALU.mult))
                link(tt(tmp[:], bank[3][:, 0:NT * E].rearrange("p (t e) -> p t e", e=E), over_t(nblk[:]), ALU.add))
                for k in range(2):
                    link(tt(oh[:, k], oh[:, k], tmp[:], ALU.mult))
                with nc.allow_low_precision(reason="sums of whole numbers, exact in float32"):
                    link(red(slot[:], oh[:], AX.X, ALU.add))
                link(tt(incl[0:1, 0:E - 1], base[0:1, 1:E], base[0:1, 1:E], ALU.max))
                ends = big[0:1, 0:NB * (E - 1)].rearrange("p (b e) -> p b e", e=E - 1)
                link(tt(ends, incl[:, None, 0:E - 1].to_broadcast([1, NB, E - 1]),
                        bno[:].unsqueeze(2).to_broadcast([1, NB, E - 1]), ALU.is_le))
                with nc.allow_low_precision(reason="sums of whole numbers, exact in float32"):
                    link(red(bex[:], ends, AX.X, ALU.add))
                dve.tensor_scalar(bexi[:, 0:NB], bex[:], float(WE), None, ALU.mult).then_inc(s_slot, 1)

            def hidden(j, par):
                dve.wait_ge(s_sg, j + 1)

            def times_up(j, par, first):
                dve.wait_ge(s_sg, j + 1)
                if not first:
                    dve.wait_ge(s_ht, j - 1)
                dve.tensor_tensor(hm[par][:], sg[par][:], bank[2 + par][:, F:GU], ALU.mult).then_inc(s_hm, 1)

            def hidden_low(j, par):
                dve.wait_ge(s_hth, j + 1)
                dve.tensor_tensor(hT[par][1][:], bank[4 + par][:, 0:P], hT[par][0][:].bitcast(F32), ALU.subtract)\
                    .then_inc(s_htl, 1)

            def ffn(f):
                route(f)
                for i in range(NT + 3):
                    j = f * NJ + i
                    if i < NT:
                        times_up(j, j % 2, f == 0 and i < 2)
                    if 0 <= i - 1 < NT:
                        hidden_low(j - 1, (j - 1) % 2)
                    if 0 <= i - 3 < NT:
                        dve.wait_ge(s_y, j - 2)
                        dve.scalar_tensor_tensor(out=res[:, i - 3, :], in0=bank[6 + (j - 3) % 2][:, 0:D], scalar=0.5,
                                                 in1=res[:, i - 3, :], op0=ALU.mult, op1=ALU.add).then_inc(s_ysh, 1)
                    if f == 0 and i + 2 < len(VEC_LOWS):
                        split_low(i + 2)

                def step(b, live):
                    j = f * NJ + NT + b
                    if live[0]:
                        dve.wait_ge(s_xth, f * NB + b + 1)
                        dve.tensor_tensor(xT[b % 2][1][:], bank[b % 2][:, 0:D].rearrange("p (k t) -> p k t", k=KT),
                                          xT[b % 2][0][:].bitcast(F32), ALU.subtract).then_inc(s_xtl, 1)
                    if live[1]:
                        times_up(j - 1, (j - 1) % 2, b - 1 >= 2)
                    if live[2]:
                        hidden_low(j - 2, j % 2)
                    if live[3]:
                        r = (b - 3) % RING
                        dve.wait_ge(s_y, j - 2)
                        if f or b - 3 >= RING:
                            dve.wait_ge(s_ys[r], 16 * ((NB - r + RING - 1) // RING * f + (b - 3) // RING))
                        dve.tensor_copy(ysb[r][:], bank[6 + (j - 3) % 2][:, 0:D]).then_inc(s_ye, 1)

                over_blocks(step)
                dve.wait_ge(s_ysh, NT * (f + 1))

            def combine(f, t):
                dve.wait_ge(s_yg[t % 4], 32 * (2 * f + t // 4 + 1))
                link(dve.scalar_tensor_tensor(out=res[:, t, :], in0=yg[t % 4][:, 0, :], scalar=gate[:, 0, t:t + 1],
                                              in1=res[:, t, :], op0=ALU.mult, op1=ALU.add))
                dve.scalar_tensor_tensor(out=res[:, t, :], in0=yg[t % 4][:, 1, :], scalar=gate[:, 1, t:t + 1],
                                         in1=res[:, t, :], op0=ALU.mult, op1=ALU.add).then_inc(s_cmb, 1)

            norm(0, 0, lambda r: dve.wait_ge(s_x[r], 16))
            dve.wait_ge(s_rw, 1)
            dve.tensor_tensor(rw[1][:], rw_s[:], rw[0][:].bitcast(F32), ALU.subtract).then_inc(s_rw, 1)
            for i in range(2):
                split_low(i)
            ffn(0)

            def part_rest(it):
                m, op = it // 2 % 2, it % 2
                dve.wait_ge(s_ph, it + 1)
                if it >= 2:
                    dve.wait_ge(s_pl, it - 1)
                dve.scalar_tensor_tensor(out=pq[it % 2][:], in0=bank[2 + it % 2][:], scalar=qkb[:, op, m:m + 1],
                                         in1=part[it % 5][:, 0, :], op0=ALU.add, op1=ALU.subtract)\
                    .then_inc(s_pr, 1)
                dve.wait_ge(s_pr, it + 1)
                dve.tensor_copy(part[it % 5][:, 1, :], pq[it % 2][:]).then_inc(s_pm, 1)

            def v_rows(c):
                for t in range(c * QT, (c + 1) * QT):
                    dve.wait_ge(s_vp, t + 1)
                    to = V[:, t, 0:H * VW].rearrange("p (h w) -> p h w", w=VW)[:, :, 0:HD]
                    dve.tensor_tensor(to, bank[4 + t % 2][:, 0:D].rearrange("p (h w) -> p h w", w=HD),
                                      vb[:].rearrange("p (h w) -> p h w", w=HD), ALU.add).then_inc(s_v, 1)

            for t in (0, 1):
                combine(0, t)
            dve.wait_ge(s_cmb, 2)
            statistics(0)
            combine(0, 2)
            normal_rows(1, 0)
            turn_low(1, 0)
            combine(0, 3)
            dve.wait_ge(s_cmb, 4)
            statistics(1)
            normal_rows(1, 1)
            combine(0, 4)
            turn_low(1, 1)
            combine(0, 5)
            dve.wait_ge(s_cmb, 6)
            statistics(2)
            normal_rows(1, 2)
            part_rest(0)
            part_rest(1)
            combine(0, 6)
            part_rest(2)
            combine(0, 7)
            dve.wait_ge(s_cmb, 8)
            statistics(3)
            normal_rows(1, 3)
            part_rest(3)
            turn_low(1, 2)
            turn_low(1, 3)
            dve.wait_ge(s_vone, 1)
            v_rows(0)
            for it in range(4, 8):
                part_rest(it)
            v_rows(1)

            def maximum(n, i):
                g, num = n // G, QT * n + QT - 1 - i
                dve.wait_ge(s_s, num + 1)
                w = (i + 1) * P
                dve.tensor_tensor_reduce(junk[num % 3][:, 0:w], bank[s_bank[num % 3]][:, 0:w], dec[:, 512 - w:512], 1.0, NEG,
                                         ALU.add, ALU.max, mmax[g % 2][:, n % G * QT + i:n % G * QT + i + 1])\
                    .then_inc(s_max, 1)

            def normalise(g):
                c, hg = g // 4, g % 4
                if g == 0:
                    dve.wait_ge(s_pd[3], 16)
                    dve.wait_ge(s_pd[4], 16)
                dve.wait_ge(s_otr, g + 1)
                src = bank[7][:].rearrange("p (i u w) -> p i u w", i=QT, w=32)
                link(dve.reciprocal(rc[:], src[:, :, :, HD]))
                to = att[:, c * QT:(c + 1) * QT, hg * G * HD:(hg + 1) * G * HD].rearrange("p i (u w) -> p i u w", w=HD)
                dve.tensor_tensor(to, src[:, :, :, 0:HD], rc[:].unsqueeze(3).to_broadcast([P, QT, G, HD]), ALU.mult)\
                    .then_inc(s_att, 1)

            def maxima_out(n):
                if n % G == 0 and G <= n <= NH:
                    g = n // G - 1
                    dve.wait_ge(s_mt, g + 1)
                    if g >= 2:
                        dve.wait_ge(s_mr[g % 2], 16 * (g // 2))
                    dve.tensor_copy(mT[g % 2][:], bank[7][:].bitcast(BF16)[0:2 * G * QT, 0:P]).then_inc(s_mts, 1)

            dve.wait_ge(s_pl, 8)
            dve.wait_ge(s_const, 3)
            for n in range(-LEAD, NH + G + 1):
                ahead = n + LEAD
                if 0 <= ahead < NH:
                    for i in range(QT):
                        if i == 2:
                            maxima_out(ahead)
                        maximum(ahead, QT - 1 - i)
                else:
                    maxima_out(ahead)
                if ahead % G == G - 1 and ahead < NH:
                    g = ahead // G
                    if g >= 2:
                        dve.wait_ge(s_mt, g - 1)
                    dve.wait_ge(s_max, QT * (ahead + 1))
                    link(dve.tensor_scalar(negm[g % 2][:, 0, :], mmax[g % 2][:], -1.0, None, ALU.mult))
                    dve.scalar_tensor_tensor(out=negm[g % 2][:, 1, :], in0=mmax[g % 2][:], scalar=-1.0,
                                             in1=negm[g % 2][:, 0, :], op0=ALU.mult, op1=ALU.subtract)\
                        .then_inc(s_nm, 1)
                if n % G == 0 and n >= 2 * G:
                    normalise(n // G - 2)
            for r in range(NP_):
                turn_low(2, r)
            dve.wait_ge(s_resb, NT)

            def projected(r):
                for t in (2 * r, 2 * r + 1):
                    dve.wait_ge(s_o, t + 1)
                    dve.tensor_tensor(res[:, t, :], bank[2 + t % 2][:, 0:D], res[:, t, :], ALU.add)\
                        .then_inc(s_res2, 1)
                dve.wait_ge(s_res2, 2 * r + 2)

            norm(2, 3, projected)
            ffn(1)
            for t in range(NT):
                combine(1, t)


_INS = ["x", "q_w", "k_w", "v_w", "o_w", "qk_b", "v_b", "o_b", "r_w", "r_b", "experts"]


def _by_partition(a):
    return a.reshape(-1, P, a.shape[1]).transpose(1, 0, 2)


def _heads_inside(a):
    b = a.reshape(a.shape[:-1] + (-1, 8, 16))
    return b.swapaxes(-1, -2).reshape(a.shape)


def kernel(**inputs):
    import numpy as np
    import concourse.bacc as bacc
    from concourse.bass_utils import run_bass_kernel_spmd

    a = {name.removeprefix("L0_"): np.asarray(v) for name, v in inputs.items()}
    given = {"x": a["attn_x"], "v_b": a["attn_v_b"], "o_b": a["attn_o_b"], "r_b": a["ffn_bias"]}
    for i in "qkvo":
        given[f"{i}_w"] = _by_partition(a[f"attn_{i}_w"].T)
    given["q_w"], given["k_w"] = (_heads_inside(given[f"{i}_w"]) for i in "qk")
    given["r_w"] = _by_partition(a["ffn_Wr"].T)
    given["qk_b"] = np.stack([_heads_inside(a[f"attn_{i}_b"]).reshape(-1, P) for i in "qk"]).transpose(2, 0, 1)
    g, u, d = (np.concatenate([a[f"ffn_W{i}"], a[f"ffn_sW{i}"][None]]) for i in "gud")
    n = len(g)
    gu = np.stack([w.reshape(n, -1, P, w.shape[2]) for w in (g, u)], axis=3)
    gu = gu.transpose(0, 2, 1, 3, 4).reshape(n, P, -1)
    given["experts"] = np.concatenate([gu, d], axis=2)
    nc = bacc.Bacc("TRN2", target_bir_lowering=False, num_devices=1)
    arrays, args = {}, []
    for name in _INS:
        arrays[f"in_{name}"] = v = np.ascontiguousarray(given[name])
        args.append(nc.dram_tensor(f"in_{name}", v.shape, mybir.dt.from_np(v.dtype), kind="ExternalInput").ap())
    args.append(nc.dram_tensor("out", given["x"].shape, F32, kind="ExternalOutput").ap())
    macaron_kernel(nc, *args)
    r = run_bass_kernel_spmd(nc, [arrays], core_ids=[0])
    return r.results[0]["out"]
```

```python
from contextlib import ExitStack

import concourse.bass as bass
from concourse import mybir

ALU = mybir.AluOpType
ACT = mybir.ActivationFunctionType
AX = mybir.AxisListType
F32 = mybir.dt.float32
F32R = mybir.dt.float32r
BF16 = mybir.dt.bfloat16
I32 = mybir.dt.int32
U32 = mybir.dt.uint32

P = 128
NEG = -3.0e38


def macaron_kernel(nc, x, q_w, k_w, v_w, o_w, qk_b, v_b, o_b, r_w, r_b, experts, masks, out):
    B, SEQ, D = x.shape
    E = experts.shape[0] - 1
    F = experts.shape[2] // 6
    N = B * SEQ
    NT = N // P
    KT = D // P
    NP_ = NT // 2
    H, HD = 16, 16
    QT = SEQ // P
    NB = (2 * N + E * (P - 1)) // P
    G = 4
    NG = B * H // G
    RING = 4
    PEEL = 5
    EPS_LN, EPS_TOP = 1e-5, 1e-9
    WE = KT * 2 * F + D
    GU = 2 * F
    XW = D + 1
    NOWHERE = 1 << 29
    STK = 6 * HD
    STM = STK + 2
    STD = STM + 3
    VW = HD + 1
    assert (P, KT, F, NB, QT) == (128, 2, 128, 31, 4)

    x_v = x.rearrange("b (t p) d -> p (b t) d", p=P)
    out_v = out.rearrange("b (t p) d -> p (b t) d", p=P)
    slots_x = nc.dram_tensor("slots_x", (NB * P, XW), F32, kind="Internal").ap()
    results = nc.dram_tensor("results", (2 * 2 * N, D), F32, kind="Internal").ap()
    parts_d = nc.dram_tensor("parts_d", (2, KT, B, 3, P, SEQ), BF16, kind="Internal").ap()

    with ExitStack() as ctx:
        def sb(name, shape, dt=F32, to=ctx):
            return to.enter_context(nc.sbuf_tensor(name, shape, dt))

        def sem(name):
            return ctx.enter_context(nc.semaphore(name))

        bank = [ctx.enter_context(nc.psum_tensor(f"bank{i}", [P, 512], F32)) for i in range(8)]

        wh = sb("wh", [P, E + 1, WE], F32R)
        r0 = ExitStack()
        w_raw = sb("w_raw", [P, E + 1, WE], F32, r0)
        r0.close()
        wl = sb("wl", [P, E + 1, WE], F32R)
        rw = [sb(f"rw_{i}", [P, KT, E], F32R) for i in "hl"]
        rw_s = sb("rw_s", [P, KT, E])
        res = sb("res", [P, NT, D])
        xn = sb("xn", [P, NT, XW])
        att = xn
        to_row = sb("to_row", [P, 4, NT], I32)
        ident = sb("ident", [P, P])
        ident_b = sb("ident_b", [P, P], BF16)
        ones_b = sb("ones_b", [P, P], BF16)
        below_b = sb("below_b", [P, P], BF16)
        stats = sb("stats", [P, NT, 6])
        mv = sb("mv", [P, NT, 2])
        rstd = sb("rstd", [P, NT])
        dev = sb("dev", [P, NT])
        warm = sb("warm", [P, 8])
        eps = sb("eps", [P, 1])
        dec = sb("dec", [P, SEQ + 1])
        dec_b = dec[:, SEQ:SEQ + 1]
        dec_d = sb("dec_d", [P, P], BF16)
        rows_k = sb("rows_k", [3, SEQ], BF16)
        rows_q = sb("rows_q", [5, SEQ], BF16)
        qkb = sb("qkb", [P, 2, KT])
        vb = sb("vb", [P, D])
        ob = sb("ob", [P, D])
        rb = sb("rb", [P, E])
        dn = sb("dn", [P, E])
        kk = sb("kk", [P, NT])
        lt = sb("lt", [P, E, E], BF16)
        bno = sb("bno", [1, NB])
        mx = sb("mx", [P, NT])
        rsum = sb("rsum", [P, NT])
        top = sb("top", [P, 2, NT])
        fst = sb("fst", [P, NT])
        gate = sb("gate", [P, 2, NT])
        nblk = sb("nblk", [P, E])
        base = sb("base", [P, E])
        incl = sb("incl", [1, E])
        bex = sb("bex", [1, NB])
        bexi = sb("bexi", [1, NB + 1], I32)
        slot = sb("slot", [P, 2, NT], U32)

        r1 = ExitStack()
        xnT = [sb(f"xnT_{i}", [P, KT, N], F32R, r1) for i in "hl"]
        r1.close()
        r1 = ExitStack()
        sb("below_wa", [P, 2 * KT * N], F32, r1)
        r0 = ExitStack()
        wa_raw = [sb(f"wa_raw{j}", [P, KT, D], F32, r0) for j in "qkv"]
        r0.close()
        wa_l = [sb(f"wa{j}_l", [P, KT, D], F32R, r1) for j in "qkv"]
        wa = [[sb(f"wa{j}_h", [P, KT, D], F32R, r1), wa_l[j]] for j in range(3)]
        r1.close()
        ct = [sb(f"ct{i}", [P, 1280]) for i in range(6)]
        r2 = ExitStack()
        r0 = ExitStack()
        masks_s = sb("masks_s", [P, P + SEQ], F32, r0)
        r0.close()
        yg = [sb(f"yg{i}", [P, 2, D], F32, r2) for i in range(4)]
        r0 = ExitStack()
        yg += [sb(f"yg{i}", [P, 2, D], F32, r0) for i in range(4, NT)]
        r0.close()
        xb = [sb(f"xb{i}", [P, XW], F32, r2) for i in range(RING)]
        yi = [sb(f"yi{i}", [P, 1], U32, r2) for i in range(2 * RING)]
        xT = [[sb(f"xT{j}_{i}", [P, KT, P], F32R, r2) for i in "hl"] for j in range(2)]
        sg = [sb(f"sg{i}", [P, F], F32, r2) for i in range(2)]
        hm = [sb(f"hm{i}", [P, F], F32, r2) for i in range(2)]
        hT = [[sb(f"hT{j}_{i}", [P, P], F32R, r2) for i in "hl"] for j in range(2)]
        ysb = [sb(f"ysb{i}", [P, D], F32, r2) for i in range(RING)]
        zeros = sb("zeros", [P, XW], F32, r2)
        lgT = sb("lgT", [E, N], F32, r2)
        lg = sb("lg", [P, NT, E], F32, r2)
        pr = sb("pr", [P, NT, E], F32, r2)
        tmp = sb("tmp", [P, NT, E], F32, r2)
        oh = sb("oh", [P, 2, NT, E], F32, r2)
        ohs = sb("ohs", [P, NT, E], BF16, r2)
        big = sb("big", [P, NB * E], F32, r2)
        iota_i = sb("iota_i", [P, 512], I32, r2)
        r2.close()
        r3 = ExitStack()
        sb("below_xo", [P, 4 * G * SEQ], BF16, r3)
        xo = [sb(f"xo_{i}", [P, KT, SEQ], F32R, r3) for i in "hl"]
        r3.close()
        stk_k, stk_q = [], []
        for i in range(3):
            stk_k.append(sb(f"stk_k{i}", [STD, G, SEQ], BF16))
            stk_q.append(sb(f"stk_q{i}", [STD, G, SEQ], BF16))
        r4 = ExitStack()
        negm = [sb(f"negm{i}", [P, 2, G * QT], BF16, r4) for i in range(2)]
        mmax = [sb(f"mmax{i}", [P, G * QT], F32, r4) for i in range(2)]
        mT = [sb(f"mT{i}", [2 * G * QT, P], BF16, r4) for i in range(2)]
        rc = sb("rc", [P, QT, G], F32, r4)
        r3 = ExitStack()
        pq = [sb(f"pq{i}", [P, 512], F32, r3) for i in range(2)]
        part = [sb(f"part{j}", [P, 3, SEQ], BF16, r3) for j in range(3)]
        for t in (0, NT // 2):
            part.append(xn[:, t:t + 4, :].rearrange("p t d -> p (t d)")[:, 0:3 * SEQ // 2].bitcast(BF16)
                        .rearrange("p (i t) -> p i t", i=3))
        r3.close()
        r3 = ExitStack()
        osb = [sb(f"osb{i}", [P, 512], F32, r3) for i in range(2)]
        wo_h = sb("wo_h", [P, KT, D], F32R, r3)
        r0 = ExitStack()
        wo_raw = sb("wo_raw", [P, KT, D], F32, r0)
        r0.close()
        wo = [wo_h, sb("wo_l", [P, KT, D], F32R, r3)]
        r3.close()
        r4.close()
        sb("below_v", [P, 3584], F32)
        V = sb("V", [P, NT, H * VW + 16])

        s_x = [sem(f"s_x{r}") for r in range(NP_)]
        s_small = sem("s_small")
        s_const = sem("s_const")
        s_w = [sem(f"s_w{q}") for q in range(E + 1)]
        s_whi = sem("s_whi")
        s_wlo_p = sem("s_wlo_p")
        s_wlo_v = sem("s_wlo_v")
        s_rw = sem("s_rw")
        s_zero = sem("s_zero")
        s_fill = sem("s_fill")
        s_dv = sem("s_dv")
        s_pool = sem("s_pool")
        s_mv = sem("s_mv")
        s_dev = sem("s_dev")
        s_xn = sem("s_xn")
        s_tr = sem("s_tr")
        s_thi = sem("s_thi")
        s_tlo = sem("s_tlo")
        s_rt = sem("s_rt")
        s_lt = sem("s_lt")
        s_lr = sem("s_lr")
        s_lg = sem("s_lg")
        s_ex = sem("s_ex")
        s_oh = sem("s_oh")
        s_cnt = sem("s_cnt")
        s_rk = sem("s_rk")
        s_slot = sem("s_slot")
        s_bex = sem("s_bex")
        s_sc = [sem(f"s_sc{i}") for i in range(4)]
        s_to = sem("s_to")
        s_xb = [sem(f"s_xb{i}") for i in range(RING)]
        s_xt = sem("s_xt")
        s_xth = sem("s_xth")
        s_xtl = sem("s_xtl")
        s_gu = sem("s_gu")
        s_sg = sem("s_sg")
        s_hm = sem("s_hm")
        s_ht = sem("s_ht")
        s_hth = sem("s_hth")
        s_htl = sem("s_htl")
        s_y = sem("s_y")
        s_ysh = sem("s_ysh")
        s_ye = sem("s_ye")
        s_yi = sem("s_yi")
        s_ys = [sem(f"s_ys{i}") for i in range(RING)]
        s_yg = [sem(f"s_yg{i}") for i in range(NT)]
        s_cm0 = sem("s_cm0")
        s_cmb = sem("s_cmb")
        s_was = [sem(f"s_was{i}") for i in range(3)]
        s_wah = sem("s_wah")
        s_wap = sem("s_wap")
        s_qkb = sem("s_qkb")
        s_vone = sem("s_vone")
        s_msk = sem("s_msk")
        s_dcy = sem("s_dcy")
        s_row = sem("s_row")
        s_dec = sem("s_dec")
        s_resb = sem("s_resb")
        s_qk = sem("s_qk")
        s_ph = sem("s_ph")
        s_pr = sem("s_pr")
        s_pm = sem("s_pm")
        s_pl = sem("s_pl")
        s_pd = [sem(f"s_pd{i}") for i in range(8)]
        s_vp = sem("s_vp")
        s_v = sem("s_v")
        s_stk = [sem(f"s_stk{i}") for i in range(3)]
        s_s = sem("s_s")
        s_max = sem("s_max")
        s_nm = sem("s_nm")
        s_mt = sem("s_mt")
        s_mts = sem("s_mts")
        s_mr = [sem(f"s_mr{i}") for i in range(2)]
        s_st = sem("s_st")
        s_exp = sem("s_exp")
        s_pv = sem("s_pv")
        s_ot = sem("s_ot")
        s_otr = sem("s_otr")
        s_att = sem("s_att")
        s_wos = sem("s_wos")
        s_wo = sem("s_wo")
        s_o = sem("s_o")
        s_res2 = sem("s_res2")
        s_out = sem("s_out")

        order = [E] + list(range(E))
        EARLY = 8
        POOL_LOWS = range(2, EARLY)
        VEC_LOWS = [q for q in range(E + 1) if q not in POOL_LOWS]
        NJ = NT + NB
        behind = {0: (3, 0), 2: (3, 384), 1: (4, 0)}
        off = [512, 1024, 896]
        LEAD = 6
        s_bank = [0, 1, 5]
        v_bank = [4, 6, 5, 7] * 2
        o_bank = [(5, 1), (2, 3)]
        NH = B * H

        def three(eng, to, xs, ws, ins):
            terms = [(k, a, b) for k in range(KT) for a, b in ((0, 0), (0, 1), (1, 0))] if ins is None else ins
            for i, (k, a, b) in enumerate(terms):
                mm = eng.matmul(to, xs(k, a), ws(k, b), start=i == 0, stop=i == len(terms) - 1)
            return mm

        turns = [(n, r) for n in (0, 1) for r in range(NT // 2)]
        turns += [(2, 0), (2, 1), (3, 0), (3, 1), (2, 2), (2, 3), (3, 2), (3, 3)]

        def number(n, r):
            return turns.index((n, r)) + 1

        def turn_bank(n, r):
            return bank[r % 2 + (2 if n == 3 and r < 2 else 0)]

        def turned(n, r, i):
            to, at = (xo, 2 * P * r) if n == 2 and r < 2 else (xnT, 2 * P * r)
            return to[i][:, :, at:at + 2 * P]

        def back(q, r, k):
            return q + (r - k) // RING, (r - k) % RING

        def over_blocks(step):
            for b in range(NB + 3):
                step(b, [0 <= b - k < NB for k in range(4)])

        block = ctx.enter_context(nc.Block())

        @block.sync
        def _(sp):
            def load_x(r):
                sp.dma_start(res[:, 2 * r:2 * r + 2, :], x_v[:, 2 * r:2 * r + 2, :]).then_inc(s_x[r], 16)

            def load_expert(q):
                sp.dma_start(w_raw[:, order[q], :], experts[order[q]]).then_inc(s_w[q], 16)

            for r in range(NP_):
                load_x(r)
            sp.dma_start(rw_s[:], r_w).then_inc(s_small, 16)
            sp.dma_start(rb[:], r_b.partition_broadcast(P)).then_inc(s_small, 16)
            sp.dma_start(qkb[:], qk_b).then_inc(s_small, 16)
            sp.dma_start(vb[:], v_b.partition_broadcast(P)).then_inc(s_small, 16)
            sp.dma_start(ob[:], o_b.partition_broadcast(P)).then_inc(s_small, 16)
            at = SEQ + 1
            sp.dma_start(masks_s[:, 0:P], masks[:, at:at + P]).then_inc(s_msk, 16)
            sp.dma_start(masks_s[0:3, P:P + SEQ], masks[0:3, at + P:at + P + SEQ]).then_inc(s_msk, 16)
            sp.dma_start(masks_s[32:37, P:P + SEQ], masks[3:8, at + P:at + P + SEQ]).then_inc(s_msk, 16)
            for q in range(EARLY):
                load_expert(q)
            sp.wait_ge(s_zero, 3)
            sp.dma_start(slots_x.rearrange("(p a) d -> p a d", p=P),
                         zeros[:, None, :].to_broadcast([P, NB, XW])).then_inc(s_fill, 16)
            for q in range(EARLY, EARLY + 3):
                load_expert(q)
            for q, (gate_sem, count) in zip(range(EARLY + 3, E + 1, 2), ((s_to, 2), (s_sc[0], 8 * NT), (s_to, 3))):
                sp.wait_ge(gate_sem, count)
                load_expert(q)
                load_expert(q + 1)
            def blocks(f):
                def load(q, r):
                    sp.dma_start(xb[r][:], slots_x[bass.ds((q * RING + r) * P, P), :]).then_inc(s_xb[r], 16)

                def step(q, r):
                    sp.wait_ge(s_xt, q * RING + (r + f * NB + 1))
                    sp.wait_ge(s_yi, q * RING + (r + f * NB + 1))
                    load(q + 1, r)

                for i in range(4):
                    sp.wait_ge(s_sc[i], 16 * NT // 2 * (f + 1))
                for b in range(RING):
                    load(0, b)
                if f == 0:
                    for j, w in enumerate((q_w, k_w, v_w)):
                        sp.dma_start(wa_raw[j][:], w).then_inc(s_was[j], 16)
                    sp.dma_start(dec[:], masks[:, 0:at]).then_inc(s_dcy, 16)
                with sp.Fori(0, NB // RING - 1) as n:
                    for r in range(RING):
                        step(n, r)
                for r in range(NB % RING):
                    step(NB // RING - 1, r)

            def load_results(f):
                for r in range(RING):
                    sp.wait_ge(s_ys[r], 16 * ((NB - r + RING - 1) // RING) * (f + 1))
                rows_v = results.rearrange("(f k t p) d -> f t p k d", f=2, k=2, p=P)
                for t in range(NT):
                    sp.dma_start(yg[t][:], rows_v[f, t]).then_inc(s_yg[t], 16)

            def attention():
                def store_parts(it):
                    sp.wait_ge(s_pl, it + 1)
                    c, m, op = it // 4, it // 2 % 2, it % 2
                    sp.dma_start(parts_d[op, m, c].rearrange("i p t -> p i t"), part[it % 5][:])\
                        .then_inc(s_pd[it], 16)

                def load_stacks(g):
                    c, hg = g // 4, g % 4
                    for it in (4 * c + hg // 2 * 2, 4 * c + hg // 2 * 2 + 1):
                        sp.wait_ge(s_pd[it], 16)
                    if g == 0:
                        sp.wait_ge(s_cmb, NT)
                    if g >= 3:
                        sp.wait_ge(s_st, 3 * G * (g - 2))
                    for op, stk in ((1, stk_k), (0, stk_q)):
                        row = 0
                        for a, n in ((0, 3), (1, 2), (2, 1)):
                            src = parts_d[op, hg // 2, c].rearrange("i (d h) t -> d i h t", d=HD)
                            src = src[:, :, hg % 2 * G:(hg % 2 + 1) * G, :].rearrange("d i h t -> d i (h t)")
                            src = src[:, a:a + 1, :].to_broadcast([HD, n, G * SEQ]) if op else src[:, 0:n, :]
                            dst = stk[g % 3][row:row + n * HD, :, :].rearrange("p h t -> p (h t)")
                            sp.dma_start(dst, src).then_inc(s_stk[g % 3], 16)
                            row += n * HD

                def decay_rows(i):
                    for to, own in ((stk_k[i][STM:STD, :, :], rows_k), (stk_q[i][STK:STD, :, :], rows_q)):
                        n = own.shape[0]
                        sp.dma_start(to, own[:, None, :].to_broadcast([n, G, SEQ])).then_inc(s_dec, 16)

                def store_maxima(g):
                    sp.wait_ge(s_mts, g + 1)
                    dst = stk_k[g % 3][STK:STM, :, :].rearrange("a u (i t) -> a (u i) t", t=P)
                    sp.dma_start(dst, mT[g % 2][:]).then_inc(s_mr[g % 2], 16)

                for it in (0, 1):
                    store_parts(it)
                load_stacks(0)
                for it in (2, 3, 4):
                    store_parts(it)
                load_stacks(1)
                sp.wait_ge(s_row, 3)
                for i in range(3):
                    decay_rows(i)
                for it in (5, 6, 7):
                    store_parts(it)
                store_maxima(0)
                load_stacks(2)
                store_maxima(1)
                for g in range(3, NG):
                    load_stacks(g)
                    store_maxima(g - 1)
                store_maxima(NG - 1)

            blocks(0)
            load_results(0)
            attention()
            blocks(1)
            load_results(1)
            for t in range(NT):
                sp.wait_ge(s_cmb, NT + t + 1)
                sp.dma_start(out_v[:, t, :], res[:, t, :]).then_inc(s_out, 16)
            sp.wait_ge(s_out, 16 * NT)

        @block.gpsimd
        def _(pool):
            steps = [0]

            def link(ins):
                steps[0] += 1
                ins.then_inc(s_pool, 1)
                pool.wait_ge(s_pool, steps[0])

            pool.memset(eps[:], EPS_LN).then_inc(s_zero, 1)
            pool.memset(zeros[:, 0:D], 0.0).then_inc(s_zero, 1)
            pool.memset(zeros[:, D:XW].bitcast(I32), NOWHERE).then_inc(s_zero, 1)
            link(pool.memset(ident[:], 0.0))
            pool.affine_select(out=ident[:], in_=ident[:], compare_op=ALU.not_equal, fill=1.0, base=0,
                               pattern=[[-1, P]], channel_multiplier=1).then_inc(s_const, 1)

            link(pool.iota(iota_i[:, 0:E], pattern=[[-1, E]], base=E, channel_multiplier=0))
            link(pool.tensor_copy(dn[:], iota_i[:, 0:E]))
            link(pool.iota(iota_i[:, 0:NT], pattern=[[P, NT]], base=0, channel_multiplier=0))
            link(pool.tensor_copy(kk[:], iota_i[:, 0:NT]))
            link(pool.iota(iota_i[0:1, 0:NB], pattern=[[P, NB]], base=0, channel_multiplier=0))
            link(pool.tensor_copy(bno[:], iota_i[0:1, 0:NB]))
            link(pool.memset(lt[:], float(P)))
            link(pool.affine_select(out=lt[:], in_=lt[:], compare_op=ALU.is_gt, fill=0.0, base=0,
                                    pattern=[[1, E], [-1, E]], channel_multiplier=0))
            link(pool.memset(ones_b[:], 1.0))
            link(pool.affine_select(out=below_b[:], in_=ones_b[:], compare_op=ALU.is_gt, fill=0.0, base=0,
                                    pattern=[[1, P]], channel_multiplier=-1))
            pool.tensor_copy(ident_b[:], ident[:]).then_inc(s_const, 1)
            link(pool.iota(to_row[:], pattern=[[P, 4 * NT]], base=0, channel_multiplier=1))

            def split_low(q):
                e = order[q]
                pool.wait_ge(s_whi, q + 1)
                pool.tensor_tensor(wl[:, e, :], w_raw[:, e, :], wh[:, e, :].bitcast(F32), ALU.subtract)\
                    .then_inc(s_wlo_p, 1)

            def scatter(f):
                for k in range(2):
                    for half in range(2):
                        tiles = range(half * NT // 2, (half + 1) * NT // 2)
                        if k:
                            pool.wait_ge(s_sc[half], 16 * len(tiles) * (f + 1))
                        elif half == 0:
                            pool.wait_ge(s_xn, NP_ * (2 * f + 1))
                        pool.tensor_copy(xn[:, tiles[0]:tiles[-1] + 1, D].bitcast(I32),
                                         to_row[:, 2 * f + k, tiles[0]:tiles[-1] + 1]).then_inc(s_to, 1)
                        pool.wait_ge(s_to, 4 * f + 2 * k + half + 1)
                        pool.wait_ge(s_slot, 2 * f + k + 1)
                        if f == 0 and k == 0 and half == 0:
                            pool.wait_ge(s_fill, 16)
                        for t in tiles:
                            where = bass.IndirectOffsetOnAxis(ap=slot[:, k, t:t + 1], axis=0)
                            pool.indirect_dma_start(slots_x, where, xn[:, t, :], None)\
                                .then_inc(s_sc[2 * k + half], 16)

            def scatter_results(f):
                def step(b, live):
                    if live[0]:
                        pool.wait_ge(s_xb[b % RING], 16 * (f * ((NB - b % RING + RING - 1) // RING) + b // RING + 1))
                        pool.tensor_copy(yi[b % (2 * RING)][:], xb[b % RING][:, D:XW].bitcast(U32)).then_inc(s_yi, 1)
                    if live[3]:
                        c = b - 3
                        pool.wait_ge(s_ye, f * NB + c + 1)
                        pool.wait_ge(s_yi, f * NB + c + 1)
                        where = bass.IndirectOffsetOnAxis(ap=yi[c % (2 * RING)][:], axis=0)
                        pool.indirect_dma_start(results, where, ysb[c % RING][:], None, bounds_check=4 * N - 1,
                                                oob_is_err=False).then_inc(s_ys[c % RING], 16)

                over_blocks(step)

            pool.memset(V[:], 1.0).then_inc(s_vone, 1)
            pool.wait_ge(s_small, 80)
            pool.tensor_scalar(qkb[:, 0, :], qkb[:, 0, :], HD ** -0.5, None, ALU.mult).then_inc(s_qkb, 1)
            for q in POOL_LOWS:
                split_low(q)
            scatter(0)
            scatter_results(0)

            for it in range(8):
                pool.wait_ge(s_pm, it + 1)
                pool.tensor_tensor(part[it % 5][:, 2, :], pq[it % 2][:], part[it % 5][:, 1, :], ALU.subtract)\
                    .then_inc(s_pl, 1)
            for t in range(NT):
                pool.tensor_tensor(res[:, t, :], res[:, t, :], ob[:], ALU.add).then_inc(s_resb, 1)
            for it in range(3, 8):
                pool.wait_ge(s_pd[it], 16)
            raw = wo_raw[:]
            pool.dma_start(raw, o_w).then_inc(s_wos, 16)
            pool.wait_ge(s_wos, 16)
            link(pool.tensor_copy(wo[0][:], raw))
            pool.tensor_tensor(wo[1][:], raw, wo[0][:].bitcast(F32), ALU.subtract).then_inc(s_wo, 1)

            scatter(1)
            scatter_results(1)

        @block.scalar
        def _(act):
            loads = [0]

            def load_table(func):
                act.activation(warm[:, loads[0]:loads[0] + 1], eps[:], func)
                loads[0] += 1

            def split_high(q):
                act.wait_ge(s_w[q], 16)
                act.activation(wh[:, order[q], :], w_raw[:, order[q], :], ACT.Copy).then_inc(s_whi, 1)

            def deviation(n, r):
                act.wait_ge(s_mv, NP_ * n + r + 1)
                act.activation(dev[:, 2 * r:2 * r + 2], mv[:, 2 * r:2 * r + 2, 1], ACT.Sqrt, bias=eps[:])\
                    .then_inc(s_dev, 1)

            def turn_high(n, r):
                act.wait_ge(s_tr, number(n, r))
                src = turn_bank(n, r)[:].rearrange("p (k t) -> p k t", k=KT)
                act.activation(turned(n, r, 0), src, ACT.Copy).then_inc(s_thi, 1)


            def hidden(j, par, first):
                act.wait_ge(s_gu, j + 1)
                if not first:
                    act.wait_ge(s_hm, j - 1)
                act.activation(sg[par][:], bank[2 + par][:, 0:F], ACT.Silu).then_inc(s_sg, 1)

            def hidden_high(j, par, first):
                act.wait_ge(s_ht, j + 1)
                if not first:
                    act.wait_ge(s_y, j - 1)
                act.activation(hT[par][0][:], bank[4 + par][:, 0:P], ACT.Copy).then_inc(s_hth, 1)

            def logits_out(f, i):
                act.wait_ge(s_rt, 2 * f + i + 1)
                act.activation(lgT[:, i * 512:(i + 1) * 512], bank[4 + i][0:E, :], ACT.Copy).then_inc(s_lt, 1)

            def ffn(f):
                load_table(ACT.Exp)
                act.wait_ge(s_lg, f + 1)
                act.activation(pr[:], lg[:], ACT.Exp).then_inc(s_ex, 1)
                load_table(ACT.Silu)
                if f == 0:
                    for q in range(NP_ + 3, EARLY):
                        split_high(q)
                for i in range(NT + 2):
                    if i < NT:
                        hidden(f * NJ + i, (f * NJ + i) % 2, i < 2 and not f)
                    if 0 <= i - 1 < NT:
                        hidden_high(f * NJ + i - 1, (f * NJ + i - 1) % 2, i - 1 < 2 and not f)
                    if f == 0 and EARLY + i <= E:
                        split_high(EARLY + i)
                if f == 0:
                    act.wait_ge(s_msk, 48)
                    act.activation(dec_d[:], masks_s[:, 0:P], ACT.Copy).then_inc(s_row, 1)
                    act.activation(rows_k[:], masks_s[0:3, P:P + SEQ], ACT.Copy).then_inc(s_row, 1)
                    act.activation(rows_q[:], masks_s[32:37, P:P + SEQ], ACT.Copy).then_inc(s_row, 1)

                def step(b, live):
                    j = f * NJ + NT + b
                    if live[0]:
                        act.wait_ge(s_xt, f * NB + b + 1)
                        if b < 2:
                            act.wait_ge(s_gu, j - 1)
                        act.activation(xT[b % 2][0][:], bank[b % 2][:, 0:D].rearrange("p (k t) -> p k t", k=KT),
                                       ACT.Copy).then_inc(s_xth, 1)
                    if live[1]:
                        hidden(j - 1, (j - 1) % 2, False)
                    if live[2]:
                        hidden_high(j - 2, j % 2, False)

                over_blocks(step)
                if f == 0:
                    for j in range(3):
                        act.wait_ge(s_was[j], 16)
                        act.activation(wa[j][0][:], wa_raw[j][:], ACT.Copy, scale=1.0 if j else HD ** -0.5)\
                            .then_inc(s_wah, 1)

            act.wait_ge(s_zero, 2)
            load_table(ACT.Sqrt)
            for r in range(NP_ + 2):
                if r < NP_:
                    deviation(0, r)
                if r == 2:
                    act.wait_ge(s_small, 80)
                    act.activation(rw[0][:], rw_s[:], ACT.Copy).then_inc(s_rw, 1)
                if r >= 2:
                    turn_high(0, r - 2)
                    split_high(r - 2)
            for q in (NP_, NP_ + 1):
                split_high(q)
            logits_out(0, 0)
            split_high(NP_ + 2)
            logits_out(0, 1)
            ffn(0)

            def part_high(it):
                m, op = it // 2 % 2, it % 2
                act.wait_ge(s_qk, it + 1)
                if it >= 5:
                    act.wait_ge(s_pd[it - 5], 16)
                act.activation(part[it % 5][:, 0, :], bank[2 + it % 2][:], ACT.Identity, bias=qkb[:, op, m:m + 1])\
                    .then_inc(s_ph, 1)

            load_table(ACT.Sqrt)
            act.wait_ge(s_qkb, 1)
            for r in range(3):
                deviation(1, r)
                if r < 2:
                    turn_high(1, r)

            def part_middle(it):
                act.wait_ge(s_pr, it + 1)
                act.activation(part[it % 5][:, 1, :], pq[it % 2][:], ACT.Copy).then_inc(s_pm, 1)

            part_high(0)
            part_high(1)
            part_middle(0)
            deviation(1, 3)
            turn_high(1, 2)
            part_high(2)
            part_middle(1)
            part_high(3)
            part_middle(2)
            turn_high(1, 3)
            part_middle(3)
            part_high(4)
            for it in range(5, 8):
                part_high(it)
                part_middle(it - 1)
            part_middle(7)
            load_table(ACT.Exp)

            def out_of_v(g):
                act.wait_ge(s_pv, g + 1)
                if g >= 2:
                    act.wait_ge(s_otr, g - 1)
                if g == 0:
                    for it in range(3, 8):
                        act.wait_ge(s_pd[it], 16)
                act.activation(osb[g % 2][:], bank[6][:], ACT.Copy).then_inc(s_ot, 1)

            act.wait_ge(s_dcy, 16)
            for n in range(NH):
                for i, (a, b) in enumerate(((0, 512), (512, 1024), (1024, 1280))):
                    act.wait_ge(s_st, 3 * n + i + 1)
                    if n >= 6 and i == 0:
                        act.wait_ge(s_pv, (n - 6) // G + 1)
                    act.activation(ct[n % 6][:, a:b], bank[2 + i][:, 0:b - a], ACT.Exp, bias=dec_b if i else 0.0)\
                        .then_inc(s_exp, 1)
                if n % G == 2 and n > G:
                    out_of_v(n // G - 1)
                if n - (NH - LEAD) in (0, 1):
                    turn_high(2, n - (NH - LEAD))
            load_table(ACT.Sqrt)
            for r in range(2):
                deviation(2, r)
            out_of_v(NG - 1)
            for turn in turns[10:14]:
                turn_high(*turn)
            logits_out(1, 0)
            for r in (2, 3):
                deviation(2, r)
            for r in (2, 3):
                turn_high(3, r)
            logits_out(1, 1)
            ffn(1)

        @block.tensor
        def _(pe):
            def turn(n, r):
                if r >= 2 and n < 2:
                    pe.wait_ge(s_tlo, number(n, r - 2))
                for k in range(KT):
                    for t in range(2):
                        mm = pe.transpose(turn_bank(n, r)[:, (2 * k + t) * P:(2 * k + t + 1) * P],
                                          xn[:, 2 * r + t, k * P:(k + 1) * P], ident[:])
                mm.then_inc(s_tr, 1)

            def rows(t):
                return lambda k, a: xnT[a][:, k, t * P:(t + 1) * P]

            def gate_up(j, par, first, xs, ws):
                if not first:
                    pe.wait_ge(s_hm, j - 1)
                three(pe, bank[2 + par][:, 0:GU], xs, ws, None).then_inc(s_gu, 1)

            def hidden_turn(j, par, first):
                pe.wait_ge(s_hm, j + 1)
                if not first:
                    pe.wait_ge(s_htl, j - 1)
                pe.transpose(bank[4 + par][:, 0:P], hm[par][:], ident[:]).then_inc(s_ht, 1)

            def down(j, par, wd):
                pe.wait_ge(s_htl, j + 1)
                three(pe, bank[6 + par][:, 0:D], lambda k, a: hT[par][a][:], lambda k, b: wd(b),
                      [(0, 0, 0), (0, 0, 1), (0, 1, 0)]).then_inc(s_y, 1)

            def logits(n, r):
                pe.wait_ge(s_tlo, number(n, r))
                mm = three(pe, bank[4 + r // 2][0:E, r % 2 * 2 * P:(r % 2 + 1) * 2 * P],
                           lambda k, a: rw[a][:, k, :],
                           lambda k, b: xnT[b][:, k, 2 * r * P:2 * (r + 1) * P], None)
                if r % 2:
                    mm.then_inc(s_rt, 1)

            def logits_turn(f, i):
                pe.wait_ge(s_lt, 2 * f + i + 1)
                for t in range(4 * i, 4 * i + 4):
                    mm = pe.transpose(bank[6][:, t * E:(t + 1) * E], lgT[:, t * P:(t + 1) * P], ident[0:E, 0:E])
                mm.then_inc(s_lr, 1)

            def ffn(f):
                pe.wait_ge(s_oh, f + 1)
                flat = ohs[:].rearrange("p t e -> p (t e)")
                for t in range(NT):
                    mm = pe.matmul(bank[4][:, 0:E], ones_b[:], flat[:, t * E:(t + 1) * E], start=t == 0,
                                   stop=t == NT - 1)
                mm.then_inc(s_cnt, 1)
                pe.matmul(bank[3][:, 0:NT * E], below_b[:], flat, start=True, stop=False, skip_group_check=True)
                for s in range(1, NT):
                    mm = pe.matmul(bank[3][:, s * E:NT * E], ones_b[:], flat[:, 0:(NT - s) * E], start=False,
                                   stop=s == NT - 1, skip_group_check=True)
                mm.then_inc(s_rk, 1)
                if f == 0:
                    pe.wait_ge(s_wlo_v, 1)
                pe.wait_ge(s_slot, 2 * f + 1)

                def w_s(k, b):
                    return (wh, wl)[b][:, E, k * GU:(k + 1) * GU]

                for i in range(NT + 2):
                    j = f * NJ + i
                    if i < NT:
                        gate_up(j, j % 2, f == 0 and i < 2, rows(i), w_s)
                    if 0 <= i - 1 < NT:
                        hidden_turn(j - 1, (j - 1) % 2, f == 0 and i - 1 < 2)
                    if 0 <= i - 2 < NT:
                        if i - 2 >= 2:
                            pe.wait_ge(s_ysh, f * NT + i - 3)
                        down(j - 2, j % 2, lambda b: (wh, wl)[b][:, E, KT * GU:WE])
                pe.wait_ge(s_ysh, (f + 1) * NT)
                if f == 0:
                    pe.wait_ge(s_wlo_v, len(VEC_LOWS))
                    pe.wait_ge(s_wlo_p, len(POOL_LOWS))

                whl = [w[:].rearrange("p e n -> p (e n)") for w in (wh, wl)]
                at = {}
                pe.wait_ge(s_bex, f + 1)

                def step(b, live):
                    j, n = f * NJ + NT + b, f * NB + b
                    if b % RING == 0 and b < NB:
                        regs = [pe.alloc_register(f"expert{f}_{i}") for i in range(b, min(b + RING, NB))]
                        pe.load(regs, bexi[0:1, b:b + len(regs)])
                        for i, reg in enumerate(regs):
                            at[b + i] = pe.snap(reg, donate=True, min_val=0, max_val=(E - 1) * WE)
                    if live[0]:
                        pe.wait_ge(s_xb[b % RING], 16 * (f * ((NB - b % RING + RING - 1) // RING) + b // RING + 1))
                        if b < 2 and f:
                            pe.wait_ge(s_xtl, n - 1)
                        for k in range(KT):
                            mm = pe.transpose(bank[b % 2][:, k * P:(k + 1) * P],
                                              xb[b % RING][:, k * P:(k + 1) * P], ident[:])
                        mm.then_inc(s_xt, 1)
                    if live[1]:
                        pe.wait_ge(s_xtl, n)
                        gate_up(j - 1, (j - 1) % 2, b - 1 >= 2, lambda k, a: xT[(b - 1) % 2][a][:, k, :],
                                lambda k, c: whl[c][:, bass.ds(at[b - 1] + k * GU, GU)])
                    if live[2]:
                        hidden_turn(j - 2, j % 2, b - 2 >= 2)
                    if live[3]:
                        if f or b >= 5:
                            pe.wait_ge(s_ye, n - 4)
                        down(j - 3, (j - 3) % 2, lambda c: whl[c][:, bass.ds(at[b - 3] + KT * GU, D)])

                over_blocks(step)

            pe.wait_ge(s_const, 1)
            for r in range(NP_):
                pe.wait_ge(s_xn, r + 1)
                turn(0, r)
            pe.wait_ge(s_rw, 2)
            pe.wait_ge(s_const, 2)
            for r in range(NP_):
                logits(0, r)
            for i in range(2):
                logits_turn(0, i)
            ffn(0)

            def v_products(tiles):
                for t in tiles:
                    if t >= QT:
                        pe.wait_ge(s_v, t - QT + 1)
                    three(pe, bank[v_bank[t]][:, 0:D], rows(t), lambda k, b: wa[2][b][:, k, :], None)\
                        .then_inc(s_vp, 1)

            def qk_product(it):
                c, m, op = it // 4, it // 2 % 2, it % 2
                if it >= 2:
                    pe.wait_ge(s_pr, it - 1)
                three(pe, bank[2 + it % 2][:], lambda k, a: wa[op][a][:, k, m * P:(m + 1) * P],
                      lambda k, b: xnT[b][:, k, c * SEQ:(c + 1) * SEQ], None).then_inc(s_qk, 1)

            def score(n, i):
                g, u, num = n // G, n % G, QT * n + QT - 1 - i
                if n % G == 0 and i == QT - 1:
                    pe.wait_ge(s_stk[g % 3], 96 * (g // 3 + 1))
                if num >= 3:
                    pe.wait_ge(s_max, num - 2)
                pe.matmul(bank[s_bank[num % 3]][:, 0:(i + 1) * P], stk_k[g % 3][0:STK, u, i * P:(i + 1) * P],
                          stk_q[g % 3][0:STK, u, 0:(i + 1) * P], start=True, stop=True).then_inc(s_s, 1)

            def scores_t(n, i):
                g, u = n // G, n % G
                if n % G == 0 and i == 0:
                    pe.wait_ge(s_mr[g % 2], 16 * (g // 2 + 1))
                if n >= 1:
                    pe.wait_ge(s_exp, 3 * (n - 1) + i + 1)
                q, k = stk_q[g % 3], stk_k[g % 3]
                if i == 0:
                    pe.matmul(bank[2][:], ident_b[:], dec_d[:, None, :].to_broadcast([P, QT, P]), start=True,
                              stop=False, skip_group_check=True)
                    for j in range(QT):
                        tile = slice(j * P, (j + 1) * P)
                        mm = pe.matmul(bank[2][:, tile], q[0:STM, u, tile], k[0:STM, u, tile], start=False,
                                       stop=True, skip_group_check=True)
                else:
                    for j, (b, at) in behind.items():
                        if b == 2 + i:
                            mm = pe.matmul(bank[b][:, at:at + SEQ - (j + 1) * P], q[:, u, j * P:(j + 1) * P],
                                           k[:, u, (j + 1) * P:SEQ], start=True, stop=True)
                mm.then_inc(s_st, 1)

            def maxima_turn(g):
                pe.wait_ge(s_nm, g + 1)
                if g >= 3:
                    pe.wait_ge(s_att, g - 2)
                pe.transpose(bank[7][:].bitcast(BF16)[0:2 * G * QT, 0:P], negm[g % 2][:].rearrange("p a n -> p (a n)"),
                             ident_b[:]).then_inc(s_mt, 1)

            def times_v(g, j, behind_it):
                c, hg = g // 4, g % 4
                if (j, behind_it) == (0, False):
                    pe.wait_ge(s_exp, 3 * G * (g + 1))
                    if g >= 1:
                        pe.wait_ge(s_ot, g)
                lo, hi, at = ((j + 1) * P, SEQ, off[j]) if behind_it else (j * P, (j + 1) * P, j * P)
                for u in range(G):
                    n, h = G * g + u, G * hg + u
                    mm = pe.matmul(bank[6][32 * u:32 * u + 32, lo:hi], V[:, c * QT + j, h * VW:h * VW + 32],
                                   ct[n % 6][:, at:at + hi - lo], start=j == 0, stop=not behind_it,
                                   skip_group_check=True)
                if j == QT - 1:
                    mm.then_inc(s_pv, 1)

            v_steps = {(0, 1): ((0, False),), (0, 2): ((0, True),), (0, 3): ((1, False),),
                       (1, 0): ((1, True),), (1, 1): ((2, False), (2, True)), (1, 2): ((3, False),)}

            def out_turn(g):
                pe.wait_ge(s_ot, g + 1)
                pe.wait_ge(s_mts, min(g + 3, NG))
                if g >= 1:
                    pe.wait_ge(s_att, g)
                for i in range(QT):
                    mm = pe.transpose(bank[7][:, i * P:(i + 1) * P], osb[g % 2][:, i * P:(i + 1) * P], ident[:])
                mm.then_inc(s_otr, 1)

            for r in range(2):
                pe.wait_ge(s_xn, NP_ + r + 1)
                turn(1, r)
            pe.wait_ge(s_wap, 3)
            pe.wait_ge(s_tlo, NP_ + 2)
            for r in (2, 3):
                qk_product(2 * r - 4)
                qk_product(2 * r - 3)
                pe.wait_ge(s_xn, NP_ + r + 1)
                turn(1, r)
            v_products(range(QT))
            pe.wait_ge(s_tlo, 2 * NP_)
            for it in (4, 5):
                qk_product(it)
            v_products(range(QT, NT))
            pe.wait_ge(s_v, NT)
            for n in range(4):
                if n < 2:
                    qk_product(6 + n)
                for i in range(QT):
                    score(n, QT - 1 - i)
            pe.wait_ge(s_pr, 8)
            pe.wait_ge(s_row, 1)

            def project(t):
                if t >= 2:
                    pe.wait_ge(s_res2, t - 1)
                own = (lambda k, a: xo[a][:, k, t * P:(t + 1) * P]) if t < QT else rows(t)
                three(pe, bank[o_bank[t // QT][t % 2]][:, 0:D], own, lambda k, b: wo[b][:, k, :], None)\
                    .then_inc(s_o, 1)

            for n in range(G - LEAD, NH + G):
                ahead = n + LEAD
                if n == 0:
                    pe.wait_ge(s_dec, 96)
                for i in range(QT):
                    if 0 <= ahead < NH:
                        score(ahead, QT - 1 - i)
                    if 0 <= n < NH and i:
                        scores_t(n, i - 1)
                    if i == 1 and ahead % G == 0 and G <= ahead <= NH:
                        maxima_turn(ahead // G - 1)
                    if n >= G:
                        for j, behind_it in v_steps.get((n % G, i), ()):
                            times_v(n // G - 1, j, behind_it)
                if n == NH + 3:
                    pe.wait_ge(s_xn, 2 * NP_ + 1)
                    turn(3, 0)
                if n % G == 3 and n > G:
                    out_turn(n // G - 1)
                if n == NH - LEAD:
                    pe.wait_ge(s_att, 4)
                    pe.wait_ge(s_max, QT * NH)
                    for r in range(2):
                        turn(2, r)
                if n == NH - LEAD + 2:
                    pe.wait_ge(s_tlo, 2 * NP_ + 2)
                    pe.wait_ge(s_wo, 1)
                    project(0)
                    project(1)
                if n == NH - LEAD + 4:
                    project(2)
                    project(3)

            pe.wait_ge(s_xn, 2 * NP_ + 2)
            turn(3, 1)
            for r in (2, 3):
                pe.wait_ge(s_att, NG)
                if r == 3:
                    pe.wait_ge(s_res2, QT)
                turn(2, r)
            for r in (0, 1):
                logits(3, r)
            pe.wait_ge(s_tlo, number(2, 3))
            for t in range(QT, NT):
                project(t)
            logits_turn(1, 0)
            for r in (2, 3):
                pe.wait_ge(s_xn, 2 * NP_ + r + 1)
                turn(3, r)
            for r in (2, 3):
                logits(3, r)
            logits_turn(1, 1)
            ffn(1)

        @block.vector
        def _(dve):
            steps = [0]

            def link(ins):
                steps[0] += 1
                ins.then_inc(s_dv, 1)
                dve.wait_ge(s_dv, steps[0])

            def split_low(i):
                q = VEC_LOWS[i]
                e = order[q]
                dve.wait_ge(s_whi, q + 1)
                dve.tensor_tensor(wl[:, e, :], w_raw[:, e, :], wh[:, e, :].bitcast(F32), ALU.subtract)\
                    .then_inc(s_wlo_v, 1)

            def statistics(r):
                for t in (2 * r, 2 * r + 1):
                    ins = dve.bn_stats(stats[:, t, :], res[:, t, :])
                link(ins)
                for t in (2 * r, 2 * r + 1):
                    ins = dve.bn_aggr(mv[:, t, :], stats[:, t, :])
                ins.then_inc(s_mv, 1)

            def normal_rows(n, r):
                dve.wait_ge(s_dev, NP_ * n + r + 1)
                link(dve.reciprocal(rstd[:, 2 * r:2 * r + 2], dev[:, 2 * r:2 * r + 2]))
                for t in (2 * r, 2 * r + 1):
                    ins = dve.tensor_scalar(xn[:, t, 0:D], res[:, t, :], mv[:, t, 0:1], rstd[:, t:t + 1],
                                            ALU.subtract, ALU.mult)
                ins.then_inc(s_xn, 1)

            def turn_low(n, r):
                dve.wait_ge(s_thi, number(n, r))
                src = turn_bank(n, r)[:].rearrange("p (k t) -> p k t", k=KT)
                dve.tensor_tensor(turned(n, r, 1), src, turned(n, r, 0).bitcast(F32), ALU.subtract).then_inc(s_tlo, 1)

            def over_e(a):
                return a.unsqueeze(2).to_broadcast([P, NT, E])

            def over_t(a):
                return a[:, None, :].to_broadcast([P, NT, E])

            def route(f):
                dve.wait_ge(s_lr, 2 * f + 2)
                if f == 0:
                    dve.wait_ge(s_const, 2)
                tt, red = dve.tensor_tensor, dve.tensor_reduce
                link(tt(lg[:], bank[6][:, 0:NT * E].rearrange("p (t e) -> p t e", e=E), over_t(rb[:]), ALU.add))
                link(red(mx[:], lg[:], AX.X, ALU.max))
                tt(lg[:], lg[:], over_e(mx[:]), ALU.subtract).then_inc(s_lg, 1)
                dve.wait_ge(s_ex, f + 1)
                for k in range(2):
                    src = pr
                    if k:
                        link(dve.scalar_tensor_tensor(out=lg[:].rearrange("p t e -> p (t e)"),
                                                      in0=oh[:, 0].rearrange("p t e -> p (t e)"), scalar=-4.0,
                                                      in1=pr[:].rearrange("p t e -> p (t e)"), op0=ALU.mult,
                                                      op1=ALU.add))
                        src = lg
                    link(red(top[:, k, :], src[:], AX.X, ALU.max))
                    link(tt(tmp[:], src[:], over_e(top[:, k, :]), ALU.is_equal))
                    link(tt(tmp[:], tmp[:], over_t(dn[:]), ALU.mult))
                    link(red(fst[:], tmp[:], AX.X, ALU.max))
                    link(tt(oh[:, k], over_t(dn[:]), over_e(fst[:]), ALU.is_equal))
                tt(ohs[:], oh[:, 0], oh[:, 1], ALU.add).then_inc(s_oh, 1)
                link(red(mx[:], pr[:], AX.X, ALU.add))
                link(dve.reciprocal(rsum[:], mx[:]))
                dve.wait_ge(s_cnt, f + 1)
                cnt = big[:, 0:E * NT].rearrange("p (e k) -> p e k", k=NT)
                link(tt(cnt, bank[4][:, 0:E].unsqueeze(2).to_broadcast([P, E, NT]),
                        kk[:, None, :].to_broadcast([P, E, NT]), ALU.is_gt))
                link(red(nblk[:], cnt, AX.X, ALU.add))
                before = big[:, 0:E * E].rearrange("p (e g) -> p e g", g=E)
                link(tt(before, nblk[:, None, :].to_broadcast([P, E, E]), lt[:], ALU.mult))
                link(red(base[:], before, AX.X, ALU.add))
                dve.wait_ge(s_rk, f + 1)
                link(tt(tmp[:], bank[3][:, 0:NT * E].rearrange("p (t e) -> p t e", e=E), over_t(base[:]), ALU.add))
                for k in range(2):
                    link(tt(oh[:, k], oh[:, k], tmp[:], ALU.mult))
                    with nc.allow_low_precision(reason="sums of whole numbers, exact in float32"):
                        red(slot[:, k], oh[:, k], AX.X, ALU.add).then_inc(s_slot, 1)
                link(tt(incl[0:1, 0:E - 1], base[0:1, 1:E], base[0:1, 1:E], ALU.max))
                ends = big[0:1, 0:NB * (E - 1)].rearrange("p (b e) -> p b e", e=E - 1)
                link(tt(ends, incl[:, None, 0:E - 1].to_broadcast([1, NB, E - 1]),
                        bno[:].unsqueeze(2).to_broadcast([1, NB, E - 1]), ALU.is_le))
                with nc.allow_low_precision(reason="sums of whole numbers, exact in float32"):
                    link(red(bex[:], ends, AX.X, ALU.add))
                dve.tensor_scalar(bexi[:, 0:NB], bex[:], float(WE), None, ALU.mult).then_inc(s_bex, 1)
                link(tt(top[:], top[:], rsum[:, None, :].to_broadcast([P, 2, NT]), ALU.mult))
                link(tt(fst[:], top[:, 0, :], top[:, 1, :], ALU.add))
                link(dve.tensor_scalar(fst[:], fst[:], EPS_TOP, None, ALU.add))
                link(dve.reciprocal(rsum[:], fst[:]))
                link(dve.scalar_tensor_tensor(out=gate[:], in0=top[:], scalar=0.5,
                                              in1=rsum[:, None, :].to_broadcast([P, 2, NT]),
                                              op0=ALU.mult, op1=ALU.mult))

            def times_up(j, par, first):
                dve.wait_ge(s_sg, j + 1)
                if not first:
                    dve.wait_ge(s_ht, j - 1)
                dve.tensor_tensor(hm[par][:], sg[par][:], bank[2 + par][:, F:GU], ALU.mult).then_inc(s_hm, 1)

            def hidden_low(j, par):
                dve.wait_ge(s_hth, j + 1)
                dve.tensor_tensor(hT[par][1][:], bank[4 + par][:, 0:P], hT[par][0][:].bitcast(F32), ALU.subtract)\
                    .then_inc(s_htl, 1)

            def ffn(f):
                route(f)
                for i in range(NT + 3):
                    j = f * NJ + i
                    if i < NT:
                        times_up(j, j % 2, f == 0 and i < 2)
                    if 0 <= i - 1 < NT:
                        hidden_low(j - 1, (j - 1) % 2)
                    if 0 <= i - 3 < NT:
                        dve.wait_ge(s_y, j - 2)
                        dve.scalar_tensor_tensor(out=res[:, i - 3, :], in0=bank[6 + (j - 3) % 2][:, 0:D], scalar=0.5,
                                                 in1=res[:, i - 3, :], op0=ALU.mult, op1=ALU.add).then_inc(s_ysh, 1)
                    if f == 0 and i + 2 < len(VEC_LOWS):
                        split_low(i + 2)

                def step(b, live):
                    j = f * NJ + NT + b
                    if live[0]:
                        dve.wait_ge(s_xth, f * NB + b + 1)
                        dve.tensor_tensor(xT[b % 2][1][:], bank[b % 2][:, 0:D].rearrange("p (k t) -> p k t", k=KT),
                                          xT[b % 2][0][:].bitcast(F32), ALU.subtract).then_inc(s_xtl, 1)
                    if live[1]:
                        times_up(j - 1, (j - 1) % 2, b - 1 >= 2)
                    if live[2]:
                        hidden_low(j - 2, j % 2)
                    if live[3]:
                        r = (b - 3) % RING
                        dve.wait_ge(s_y, j - 2)
                        if f or b - 3 >= RING:
                            dve.wait_ge(s_ys[r], 16 * ((NB - r + RING - 1) // RING * f + (b - 3) // RING))
                        dve.tensor_copy(ysb[r][:], bank[6 + (j - 3) % 2][:, 0:D]).then_inc(s_ye, 1)

                over_blocks(step)
                dve.wait_ge(s_ysh, NT * (f + 1))
                if f == 0:
                    for j in range(3):
                        dve.wait_ge(s_wah, j + 1)
                        dve.scalar_tensor_tensor(out=wa[j][1][:], in0=wa_raw[j][:], scalar=1.0 if j else HD ** -0.5,
                                                 in1=wa[j][0][:].bitcast(F32), op0=ALU.mult, op1=ALU.subtract)\
                            .then_inc(s_wap, 1)

            def combine(f, r, ks=(0, 1)):
                for k in ks:
                    for t in (2 * r, 2 * r + 1):
                        if k == 0:
                            dve.wait_ge(s_yg[t], 16 * (f + 1))
                        else:
                            dve.wait_ge(s_cm0, NT * f + t + 1)
                        dve.scalar_tensor_tensor(out=res[:, t, :], in0=yg[t][:, k, :],
                                                 scalar=gate[:, k, t:t + 1], in1=res[:, t, :], op0=ALU.mult,
                                                 op1=ALU.add).then_inc((s_cm0, s_cmb)[k], 1)

            def loaded(r):
                dve.wait_ge(s_x[r], 16)

            def router_low():
                dve.wait_ge(s_small, 80)
                dve.wait_ge(s_rw, 1)
                dve.tensor_tensor(rw[1][:], rw_s[:], rw[0][:].bitcast(F32), ALU.subtract).then_inc(s_rw, 1)

            for r in range(NP_ + 2):
                if r < NP_:
                    loaded(r)
                    statistics(r)
                if 1 <= r <= NP_:
                    normal_rows(0, r - 1)
                if r == NP_:
                    router_low()
                if r >= 2:
                    turn_low(0, r - 2)
            for i in range(2):
                split_low(i)
            ffn(0)

            def part_rest(it):
                m, op = it // 2 % 2, it % 2
                dve.wait_ge(s_ph, it + 1)
                if it >= 2:
                    dve.wait_ge(s_pl, it - 1)
                dve.scalar_tensor_tensor(out=pq[it % 2][:], in0=bank[2 + it % 2][:], scalar=qkb[:, op, m:m + 1],
                                         in1=part[it % 5][:, 0, :], op0=ALU.add, op1=ALU.subtract)\
                    .then_inc(s_pr, 1)

            def v_rows(tiles):
                for t in tiles:
                    dve.wait_ge(s_vp, t + 1)
                    to = V[:, t, 0:H * VW].rearrange("p (h w) -> p h w", w=VW)[:, :, 0:HD]
                    dve.tensor_tensor(to, bank[v_bank[t]][:, 0:D].rearrange("p (h w) -> p h w", w=HD),
                                      vb[:].rearrange("p (h w) -> p h w", w=HD), ALU.add).then_inc(s_v, 1)

            combine(0, 0)
            dve.wait_ge(s_cmb, 2)
            statistics(0)
            combine(0, 1)
            normal_rows(1, 0)
            dve.wait_ge(s_cmb, 4)
            statistics(1)
            combine(0, 2, (0,))
            normal_rows(1, 1)
            turn_low(1, 0)
            combine(0, 2, (1,))
            turn_low(1, 1)
            dve.wait_ge(s_cmb, 6)
            statistics(2)
            combine(0, 3, (0,))
            normal_rows(1, 2)
            combine(0, 3, (1,))
            part_rest(0)
            dve.wait_ge(s_cmb, 8)
            statistics(3)
            part_rest(1)
            normal_rows(1, 3)
            turn_low(1, 2)
            part_rest(2)
            part_rest(3)
            turn_low(1, 3)
            dve.wait_ge(s_vone, 1)
            v_rows(range(QT))

            def maximum(n, i):
                g, num = n // G, QT * n + QT - 1 - i
                dve.wait_ge(s_s, num + 1)
                w = (i + 1) * P
                s_i = bank[s_bank[num % 3]][:, 0:w]
                dve.tensor_tensor_reduce(s_i, s_i, dec[:, SEQ - w:SEQ], 1.0, NEG,
                                         ALU.add, ALU.max, mmax[g % 2][:, n % G * QT + i:n % G * QT + i + 1])\
                    .then_inc(s_max, 1)

            def negated(g):
                if g >= 2:
                    dve.wait_ge(s_mt, g - 1)
                dve.wait_ge(s_max, QT * G * (g + 1))
                link(dve.tensor_scalar(negm[g % 2][:, 0, :], mmax[g % 2][:], -1.0, None, ALU.mult))
                dve.scalar_tensor_tensor(out=negm[g % 2][:, 1, :], in0=mmax[g % 2][:], scalar=-1.0,
                                         in1=negm[g % 2][:, 0, :], op0=ALU.mult, op1=ALU.subtract)\
                    .then_inc(s_nm, 1)

            def normalise(g):
                c, hg = g // 4, g % 4
                if g == 0:
                    dve.wait_ge(s_pd[3], 16)
                    dve.wait_ge(s_pd[4], 16)
                dve.wait_ge(s_otr, g + 1)
                src = bank[7][:].rearrange("p (i u w) -> p i u w", i=QT, w=32)
                link(dve.reciprocal(rc[:], src[:, :, :, HD]))
                to = att[:, c * QT:(c + 1) * QT, hg * G * HD:(hg + 1) * G * HD].rearrange("p i (u w) -> p i u w", w=HD)
                dve.tensor_tensor(to, src[:, :, :, 0:HD], rc[:].unsqueeze(3).to_broadcast([P, QT, G, HD]), ALU.mult)\
                    .then_inc(s_att, 1)

            def maxima_out(n):
                if n % G == 0 and G <= n <= NH:
                    g = n // G - 1
                    dve.wait_ge(s_mt, g + 1)
                    if g >= 2:
                        dve.wait_ge(s_mr[g % 2], 16 * (g // 2))
                    dve.tensor_copy(mT[g % 2][:], bank[7][:].bitcast(BF16)[0:2 * G * QT, 0:P]).then_inc(s_mts, 1)

            dve.wait_ge(s_dcy, 16)
            part_rest(4)
            part_rest(5)
            v_rows(range(QT, NT))
            for n in range(4):
                for i in range(QT):
                    maximum(n, QT - 1 - i)
                if n < 2:
                    part_rest(6 + n)
            negated(0)

            def projected(r):
                for t in (2 * r, 2 * r + 1):
                    dve.wait_ge(s_o, t + 1)
                    dve.tensor_tensor(res[:, t, :], bank[o_bank[t // QT][t % 2]][:, 0:D], res[:, t, :], ALU.add)\
                        .then_inc(s_res2, 1)
                dve.wait_ge(s_res2, 2 * r + 2)

            for n in range(G - LEAD, NH + G + 1):
                ahead = n + LEAD
                if 0 <= ahead < NH:
                    for i in range(QT):
                        if i == 2:
                            maxima_out(ahead)
                        maximum(ahead, QT - 1 - i)
                else:
                    maxima_out(ahead)
                if ahead % G == G - 1 and ahead < NH:
                    negated(ahead // G)
                if n == NH + G:
                    for r in range(2):
                        normal_rows(2, r)
                if n % G == 0 and n >= 2 * G:
                    normalise(n // G - 2)
                if n == NH - LEAD + 1:
                    turn_low(2, 0)
                    turn_low(2, 1)
                    dve.wait_ge(s_resb, NT)
                if n - (NH - LEAD + 4) in (0, 1):
                    projected(n - (NH - LEAD + 4))
                    statistics(n - (NH - LEAD + 4))
            for turn in turns[10:14]:
                turn_low(*turn)
            projected(2)
            statistics(2)
            projected(3)
            normal_rows(2, 2)
            statistics(3)
            normal_rows(2, 3)
            for r in (2, 3):
                turn_low(3, r)
            ffn(1)
            for r in range(NP_):
                combine(1, r)


_INS = ["x", "q_w", "k_w", "v_w", "o_w", "qk_b", "v_b", "o_b", "r_w", "r_b", "experts", "masks"]


def _by_partition(a):
    return a.reshape(-1, P, a.shape[1]).transpose(1, 0, 2)


def _masks():
    import numpy as np
    p, c = np.arange(P)[:, None], np.arange(512)[None]
    behind = np.where(c - 384 <= p, c - 384.0 - p, NEG)
    diagonal = np.where(p <= c[:, :P], p - 1.0 * c[:, :P], NEG)
    rows = np.zeros((P, 512))
    tile = c[0] // P
    rows[0] = -(c[0] % P + 1)
    rows[1] = -P * np.maximum(tile - 1, 0)
    rows[2] = -P * (tile == 3)
    rows[3:6], rows[6], rows[7] = 1, tile == 0, tile == 1
    return np.concatenate([behind, p - 127.0, diagonal, rows], axis=1).astype(np.float32)


def _heads_inside(a):
    b = a.reshape(a.shape[:-1] + (-1, 8, 16))
    return b.swapaxes(-1, -2).reshape(a.shape)


def kernel(**inputs):
    import numpy as np
    import concourse.bacc as bacc
    from concourse.bass_utils import run_bass_kernel_spmd

    a = {name.removeprefix("L0_"): np.asarray(v) for name, v in inputs.items()}
    given = {"x": a["attn_x"], "v_b": a["attn_v_b"], "o_b": a["attn_o_b"], "r_b": a["ffn_bias"]}
    for i in "qkvo":
        given[f"{i}_w"] = _by_partition(a[f"attn_{i}_w"].T)
    given["q_w"], given["k_w"] = (_heads_inside(given[f"{i}_w"]) for i in "qk")
    given["r_w"] = _by_partition(a["ffn_Wr"].T)
    given["qk_b"] = np.stack([_heads_inside(a[f"attn_{i}_b"]).reshape(-1, P) for i in "qk"]).transpose(2, 0, 1)
    g, u, d = (np.concatenate([a[f"ffn_W{i}"], a[f"ffn_sW{i}"][None]]) for i in "gud")
    n = len(g)
    gu = np.stack([w.reshape(n, -1, P, w.shape[2]) for w in (g, u)], axis=3)
    gu = gu.transpose(0, 2, 1, 3, 4).reshape(n, P, -1)
    given["experts"] = np.concatenate([gu, d], axis=2)
    given["masks"] = _masks()
    nc = bacc.Bacc("TRN2", target_bir_lowering=False, num_devices=1)
    arrays, args = {}, []
    for name in _INS:
        arrays[f"in_{name}"] = v = np.ascontiguousarray(given[name])
        args.append(nc.dram_tensor(f"in_{name}", v.shape, mybir.dt.from_np(v.dtype), kind="ExternalInput").ap())
    args.append(nc.dram_tensor("out", given["x"].shape, F32, kind="ExternalOutput").ap())
    macaron_kernel(nc, *args)
    r = run_bass_kernel_spmd(nc, [arrays], core_ids=[0])
    return r.results[0]["out"]
```
